# Optimizing a Trainium2 kernel written in Bass

```python
import numpy as np
import jax
import jax.numpy as jnp

def _softmax(x, axis=-1):
    return jax.nn.softmax(x, axis=axis)

def _gelu(x):
    return jax.nn.gelu(x, approximate=True)

def _silu(x):
    return jax.nn.silu(x)

def _sigmoid(x):
    return jax.nn.sigmoid(x)

def _layernorm(x, axis=-1, eps=1e-05):
    m = jnp.mean(x, axis=axis, keepdims=True)
    v = jnp.var(x, axis=axis, keepdims=True)
    return (x - m) / jnp.sqrt(v + eps)

def _scatter_add(tgt, idx, src, axis=0):
    return tgt.at[idx].add(src)

def _segment_sum(src, seg, n):
    return jax.ops.segment_sum(src, seg, n)
kernel_name = 'mk_xattn_ffn_d1_seqx_r8_e5087b'

def setup_inputs(seed: int=0):
    np.random.seed(seed)
    _w = jnp.asarray

    def _rec_inputs():
        import jax
        import jax.numpy as jnp
        _rk = jax.random.key(seed)
        x = 7.22e-05 + 1 * jax.random.normal(jax.random.fold_in(_rk, 1), (64, 64, 128), jnp.float32)
        _lenS = 64 - jax.random.randint(jax.random.fold_in(_rk, 7), (64,), 0, max(1, 64 // 4) + 1, jnp.int32)
        _lenS2 = 64 - jax.random.randint(jax.random.fold_in(_rk, 8), (64,), 0, max(1, 64 // 4) + 1, jnp.int32)
        _ctx_1024P = jax.random.normal(jax.random.fold_in(_rk, 11), (64, 16, 128), jnp.float32)
        _ctx_1024c = jax.random.dirichlet(jax.random.fold_in(_rk, 511), 0.3 * jnp.ones((16,), jnp.float32), (64, 64))
        _ctx_1024t = jnp.einsum('bsk,bkd->bsd', _ctx_1024c, _ctx_1024P)
        _ctx_1024t = _ctx_1024t * jax.lax.rsqrt(jnp.mean(jnp.square(_ctx_1024t)) + 1e-12) * 0.953939
        ctx_1024 = 4.13588e-05 + 0.999923 * (_ctx_1024t + 0.3 * jax.random.normal(jax.random.fold_in(_rk, 611), (64, 64, 128), jnp.float32))
        _validS = jnp.arange(64)[None, :] < _lenS[:, None]
        _validS2 = jnp.arange(64)[None, :] < _lenS2[:, None]
        _causal = jnp.tril(jnp.ones((64, 64), dtype=bool))
        mask_SxS2_bk0 = jnp.logical_not(jnp.broadcast_to(_validS2[0:1, :], (64, 64)))
        return (x, ctx_1024, mask_SxS2_bk0)
    x, ctx_1024, mask_SxS2_bk0 = _rec_inputs()

    def _L0_xattn_setup():
        import jax, jax.numpy as jnp
        import numpy as np
        B, S, DIM, H = (4, 256, 128, 16)
        HD = DIM // H
        SCALE = HD ** (-0.5)

        def _heads(x):
            b, s, _ = x.shape
            return x.reshape(b, s, H, HD).transpose(0, 2, 1, 3)
        key = jax.random.key(seed)
        ks = jax.random.split(key, 7)
        init = 0.02
        return {'query': jax.random.normal(ks[0], (B, S, DIM), dtype=jnp.float32), 'key': jax.random.normal(ks[1], (B, S, DIM), dtype=jnp.float32), 'value': jax.random.normal(ks[2], (B, S, DIM), dtype=jnp.float32), 'attn_mask': jnp.tril(jnp.ones((S, S), dtype=bool)), 'Wq': jax.random.normal(ks[3], (DIM, DIM), dtype=jnp.float32) * init, 'Wk': jax.random.normal(ks[4], (DIM, DIM), dtype=jnp.float32) * init, 'Wv': jax.random.normal(ks[5], (DIM, DIM), dtype=jnp.float32) * init, 'Wo': jax.random.normal(ks[6], (DIM, DIM), dtype=jnp.float32) * init}
    _L0_xattn_all = _L0_xattn_setup()
    _L0_xattn_in = {k: v for k, v in _L0_xattn_all.items() if k in ('Wq', 'Wk', 'Wv', 'Wo')}
    del _L0_xattn_all

    def _L0_ffn_setup():
        import jax, jax.numpy as jnp
        import numpy as np
        import math
        D_MODEL = 128
        D_FF = 512
        NUM_EXPERTS = 8
        NUM_SHARED = 1
        E_ROUTED = NUM_EXPERTS - NUM_SHARED
        TOP_K = 2
        CAP_FACTOR = 1.25
        B, S = (4, 256)
        T = B * S
        CAPACITY = math.ceil(CAP_FACTOR * T * TOP_K / E_ROUTED)
        SHARED_SCALE = 1.0

        def _layernorm(x, g, b, eps=1e-05):
            mu = jnp.mean(x, axis=-1, keepdims=True)
            var = jnp.mean((x - mu) ** 2, axis=-1, keepdims=True)
            return (x - mu) * jax.lax.rsqrt(var + eps) * g + b
        key = jax.random.key(seed)
        ks = jax.random.split(key, 10)
        s = 0.02
        return {'x': jax.random.normal(ks[0], (B, S, D_MODEL), dtype=jnp.float32), 'ln_g': jnp.ones((D_MODEL,), jnp.float32), 'ln_b': jnp.zeros((D_MODEL,), jnp.float32), 'Wr': jax.random.normal(ks[1], (D_MODEL, E_ROUTED), jnp.float32) * s, 'W1': jax.random.normal(ks[2], (E_ROUTED, D_MODEL, D_FF), jnp.float32) * s, 'W3': jax.random.normal(ks[3], (E_ROUTED, D_MODEL, D_FF), jnp.float32) * s, 'W2': jax.random.normal(ks[4], (E_ROUTED, D_FF, D_MODEL), jnp.float32) * s, 'W1s': jax.random.normal(ks[5], (D_MODEL, D_FF), jnp.float32) * s, 'W3s': jax.random.normal(ks[6], (D_MODEL, D_FF), jnp.float32) * s, 'W2s': jax.random.normal(ks[7], (D_FF, D_MODEL), jnp.float32) * s}
    _L0_ffn_all = _L0_ffn_setup()
    _L0_ffn_in = {k: v for k, v in _L0_ffn_all.items() if k in ('ln_g', 'ln_b', 'Wr', 'W1', 'W3', 'W2', 'W1s', 'W3s', 'W2s')}
    del _L0_ffn_all
    return {'x': x, 'ctx_1024': ctx_1024, 'mask_SxS2_bk0': mask_SxS2_bk0, 'L0_xattn_Wq': _L0_xattn_in['Wq'], 'L0_xattn_Wk': _L0_xattn_in['Wk'], 'L0_xattn_Wv': _L0_xattn_in['Wv'], 'L0_xattn_Wo': _L0_xattn_in['Wo'], 'L0_ffn_ln_g': _L0_ffn_in['ln_g'], 'L0_ffn_ln_b': _L0_ffn_in['ln_b'], 'L0_ffn_Wr': _L0_ffn_in['Wr'], 'L0_ffn_W1': _L0_ffn_in['W1'], 'L0_ffn_W3': _L0_ffn_in['W3'], 'L0_ffn_W2': _L0_ffn_in['W2'], 'L0_ffn_W1s': _L0_ffn_in['W1s'], 'L0_ffn_W3s': _L0_ffn_in['W3s'], 'L0_ffn_W2s': _L0_ffn_in['W2s']}

def reference(x, ctx_1024, mask_SxS2_bk0, L0_xattn_Wq, L0_xattn_Wk, L0_xattn_Wv, L0_xattn_Wo, L0_ffn_ln_g, L0_ffn_ln_b, L0_ffn_Wr, L0_ffn_W1, L0_ffn_W3, L0_ffn_W2, L0_ffn_W1s, L0_ffn_W3s, L0_ffn_W2s):
    import jax
    import jax.numpy as jnp

    def _L0_xattn_ref(query, key, value, attn_mask, Wq, Wk, Wv, Wo):
        import jax, jax.numpy as jnp
        import numpy as np
        B, S, DIM, H = (4, 256, 128, 16)
        HD = DIM // H
        SCALE = HD ** (-0.5)

        def _heads(x):
            b, s, _ = x.shape
            return x.reshape(b, s, H, HD).transpose(0, 2, 1, 3)
        q = _heads(query @ Wq.T)
        k = _heads(key @ Wk.T)
        v = _heads(value @ Wv.T)
        logits = jnp.einsum('bhqd,bhkd->bhqk', q, k) * SCALE
        mask = attn_mask[None, None, :, :]
        masked = jnp.where(mask, logits, -1000000000.0)
        weights = jax.nn.softmax(masked, axis=-1)
        weights = weights * mask.astype(weights.dtype)
        denom = jnp.maximum(weights.sum(axis=-1, keepdims=True), 1e-09)
        weights = weights / denom
        out = jnp.einsum('bhqk,bhkd->bhqd', weights, v)
        out = out.transpose(0, 2, 1, 3).reshape(query.shape[0], query.shape[1], -1)
        return out @ Wo.T

    def _L0_ffn_ref(x, ln_g, ln_b, Wr, W1, W3, W2, W1s, W3s, W2s):
        import jax, jax.numpy as jnp
        import numpy as np
        import math
        D_MODEL = 128
        D_FF = 512
        NUM_EXPERTS = 8
        NUM_SHARED = 1
        E_ROUTED = NUM_EXPERTS - NUM_SHARED
        TOP_K = 2
        CAP_FACTOR = 1.25
        B, S = (4, 256)
        T = B * S
        CAPACITY = math.ceil(CAP_FACTOR * T * TOP_K / E_ROUTED)
        SHARED_SCALE = 1.0

        def _layernorm(x, g, b, eps=1e-05):
            mu = jnp.mean(x, axis=-1, keepdims=True)
            var = jnp.mean((x - mu) ** 2, axis=-1, keepdims=True)
            return (x - mu) * jax.lax.rsqrt(var + eps) * g + b
        Bx, Sx, D = x.shape
        Tn = Bx * Sx
        h = _layernorm(x, ln_g, ln_b).reshape(Tn, D)
        logits = h @ Wr
        top_vals, top_idx = jax.lax.top_k(logits, TOP_K)
        gates = jax.nn.softmax(top_vals, axis=-1)
        idx = top_idx.T.reshape(-1)
        gat = gates.T.reshape(-1)
        tok = jnp.tile(jnp.arange(Tn), TOP_K)
        onehot = jax.nn.one_hot(idx, E_ROUTED, dtype=jnp.int32)
        pos = jnp.sum(jnp.cumsum(onehot, axis=0) * onehot, axis=-1) - 1
        keep = pos < CAPACITY
        pos_c = jnp.where(keep, pos, CAPACITY)
        xe = jnp.zeros((E_ROUTED, CAPACITY, D), h.dtype).at[idx, pos_c].set(h[tok], mode='drop')
        a = jnp.einsum('ecd,edf->ecf', xe, W1)
        b = jnp.einsum('ecd,edf->ecf', xe, W3)
        ye = jnp.einsum('ecf,efd->ecd', jax.nn.silu(a) * b, W2)
        out_slots = ye[jnp.clip(idx, 0, E_ROUTED - 1), jnp.clip(pos_c, 0, CAPACITY - 1)]
        out_slots = out_slots * (gat * keep.astype(gat.dtype))[:, None]
        routed = jnp.zeros((Tn, D), h.dtype).at[tok].add(out_slots)
        shared = jax.nn.silu(h @ W1s) * (h @ W3s) @ W2s
        out = routed + SHARED_SCALE * shared
        return out.reshape(Bx, Sx, D)
    x = x + _L0_xattn_ref(_layernorm(x, axis=-1), ctx_1024, ctx_1024, mask_SxS2_bk0, L0_xattn_Wq, L0_xattn_Wk, L0_xattn_Wv, L0_xattn_Wo)
    x = x + _L0_ffn_ref(_layernorm(x, axis=-1), L0_ffn_ln_g, L0_ffn_ln_b, L0_ffn_Wr, L0_ffn_W1, L0_ffn_W3, L0_ffn_W2, L0_ffn_W1s, L0_ffn_W3s, L0_ffn_W2s)
    return x

_drawn_inputs = setup_inputs


def setup_inputs(seed=0):
    import zlib

    import numpy as np

    out = dict(_drawn_inputs(seed))
    spreads = {'L0_ffn_ln_g': (1.0, 0.6), 'L0_ffn_ln_b': (0.0, 0.8)}
    factors = {'L0_xattn_Wq': 8.0,
     'L0_xattn_Wk': 8.0,
     'L0_ffn_Wr': 8.0,
     'L0_ffn_W1': 8.0,
     'L0_ffn_W3': 8.0,
     'L0_ffn_W2': 8.0,
     'L0_ffn_W1s': 4.363,
     'L0_ffn_W3s': 4.321,
     'L0_ffn_W2s': 4.323}
    for name, (base, spread) in spreads.items():
        noise = np.random.default_rng([zlib.crc32(name.encode()), seed]).standard_normal(out[name].shape)
        drawn = base * np.exp(spread * noise) if base else spread * noise
        out[name] = jnp.asarray(drawn.astype(out[name].dtype))
    for name, factor in factors.items():
        out[name] = (out[name] * factor).astype(out[name].dtype)
    return out
```

```python
from contextlib import ExitStack

import concourse.bass as bass
from concourse import mybir

F32 = mybir.dt.float32
F16 = mybir.dt.float16
BF16 = mybir.dt.bfloat16
I32 = mybir.dt.int32
U32 = mybir.dt.uint32
U8 = mybir.dt.uint8
ALU = mybir.AluOpType
ACT = mybir.ActivationFunctionType
X = mybir.AxisListType.X

P = 128
EPS = 1e-5
CAPACITY_TOKENS = 4 * 256
TOP_K = 2
BANKS = 8
BANK = 512


def at_least(engine, semaphore, value):
    if isinstance(value, int) and value <= 0:
        return
    engine.wait_ge(semaphore, value)


class Chain:

    def __init__(self, engine, semaphore):
        self.engine, self.semaphore, self.count = engine, semaphore, 0

    def then(self, instruction):
        self.count += 1
        instruction.then_inc(self.semaphore, 1)
        self.engine.wait_ge(self.semaphore, self.count)


def xattn_moe(nc, x, ctx, mask, wq, wk, wv, wo, ln_g, ln_b, wr, w1, w3, w2, w1s, w3s, w2s, normed, out):
    B, S, D = x.shape
    T = B * S
    NT = T // P
    H = 16
    HD = D // H
    SCALE = float(HD) ** -0.5
    E, _, F = w1.shape
    FB = F // P
    CAP = -(-5 * CAPACITY_TOKENS * TOP_K // (4 * E))
    EB = -(-CAP // P)
    NB = E * EB
    G = P // 32
    J = H // G
    HH = H // 2
    CH = 4
    NC = NT // CH
    assert S * 2 == P and D == P and HH * S == BANK and NT % (2 * CH) == 0

    x_tiles = x.rearrange("b s d -> (b s) d").rearrange("(t p) d -> p t d", p=P)
    ctx_rows = ctx.rearrange("b s d -> (b s) d")
    normed_tiles = normed.rearrange("(t p) d -> p t d", p=P)
    out_tiles = out[0:T, :].rearrange("(t p) d -> p t d", p=P)

    with ExitStack() as stack:
        def sb(name, shape, dtype=F32):
            return stack.enter_context(nc.sbuf_tensor(name, shape, dtype))

        def sem(name):
            return stack.enter_context(nc.semaphore(name))

        bank = [stack.enter_context(nc.psum_tensor(f"bank{i}", [P, BANK], F32)) for i in range(BANKS)]

        w_raw = sb("w_raw", [P, 4, P])
        w_t = sb("w_t", [P, 4, P])
        wr_sb = sb("wr_sb", [P, E])
        w1_sb = sb("w1_sb", [P, E + 1, F])
        w3_sb = sb("w3_sb", [P, E + 1, F])
        w2_sb = sb("w2_sb", [P, E + 1, FB, D])
        g_col = sb("g_col", [P, 1])
        b_col = sb("b_col", [P, 1])
        ident = sb("ident", [P, P])
        q_select = sb("q_select", [P, S], BF16)
        mask_u8 = sb("mask_u8", [P, S], U8)
        mask_bias = sb("mask_bias", [P, S], BF16)
        row_any = sb("row_any", [P, 1])
        group_mask = sb("group_mask", [P, G, P], F16)
        slot_mask = sb("slot_mask", [P, J, P], F16)
        j_index = sb("j_index", [P, J, P], I32)
        p_index = sb("p_index", [P, 1], I32)
        p_head = sb("p_head", [P, 1], I32)
        p_head_f = sb("p_head_f", [P, 1])
        x_sb = sb("x_sb", [P, NT, D])
        ctx_sb = sb("ctx_sb", [P, 2, D])
        stats = sb("stats", [P, 6])
        x1_now = sb("x1_now", [P, 2, D])
        stats_now = sb("stats_now", [P, 2, 6])
        stats_all = sb("stats_all", [P, NT, 6])
        moments = sb("moments", [P, NT, 2])
        rstd = sb("rstd", [P, NT])
        newton = sb("newton", [P, NT])
        variance = sb("variance", [P, NT])
        xn = sb("xn", [P, 2, D])
        xc_t = sb("xc_t", [P, 2, P])
        qk_parts = sb("qk_parts", [P, 2, 2, P], F16)
        q_masked = sb("q_masked", [P, 2, 2, G, P], F16)
        k_masked = sb("k_masked", [P, 2, 2, J, P], F16)
        v_block = sb("v_block", [P, 2, 2, H // 2, 2, HD + 1])
        row_max = sb("row_max", [P, 2, HH])
        shifted = sb("shifted", [P, 2, HH, S])
        probs = sb("probs", [P, 2, 2, HH * S])
        probs_t = sb("probs_t", [P, 2, HH // 2, P])
        att_sum = sb("att_sum", [P, H])
        att_inv = sb("att_inv", [P, H])
        att = sb("att", [P, H, HD])
        att_t = sb("att_t", [P, P])
        t_sb = sb("t_sb", [P, 2, CH, D])
        h_now = sb("h_now", [P, 2, CH * P])
        h_t = sb("h_t", [P, NT * P])
        logits = sb("logits", [P, NT, E])
        CT = TOP_K * NT
        by_index = sb("by_index", [P, E])
        e_index = sb("e_index", [P, E])
        top = sb("top", [P, TOP_K, NT])
        eq = sb("eq", [P, NT, E])
        rest = sb("rest", [P, NT, E])
        pick = sb("pick", [P, NT])
        one_hot = sb("one_hot", [P, CT, E])
        one_hot_b = sb("one_hot_b", [P, CT, E], BF16)
        upto = sb("upto", [P, P], BF16)
        ones_b = sb("ones_b", [P, P], BF16)
        zeros = sb("zeros", [P, CT])
        totals = sb("totals", [P, CT, E])
        running = sb("running", [P, CT, E])
        place = sb("place", [P, CT, E])
        rank = sb("rank", [P, CT])
        expert = sb("expert", [P, CT])
        past1 = sb("past1", [P, CT])
        blk = sb("blk", [P, CT])
        lo = sb("lo", [P, CT])
        keep = sb("keep", [P, CT])
        lo_b = sb("lo_b", [P, CT], BF16)
        blk_b = sb("blk_b", [P, CT], BF16)
        gates = sb("gates", [P, TOP_K, NT])
        gate_e = sb("gate_e", [P, NT])
        gate_d = sb("gate_d", [P, NT])
        LC = 16
        VALS = 5
        vals = sb("vals", [P, CT, VALS], BF16)
        gate_rest = sb("gate_rest", [P, CT])
        lane = sb("lane", [P, P], BF16)
        blocks = sb("blocks", [P, NB], BF16)
        at_lane = sb("at_lane", [P, 2, LC, P], BF16)
        at_block = sb("at_block", [P, LC, NB], BF16)
        carried = sb("carried", [P, 2, LC, VALS, NB], BF16)
        table = sb("table", [P, VALS, NB])
        used = sb("used", [P, NB])
        token = sb("token", [P, NB])
        spare = sb("spare", [P, NB])
        slot_gate = sb("slot_gate", [P, NB])
        from_row = sb("from_row", [P, NB], I32)
        to_row = sb("to_row", [P, NB], I32)
        p_index_f = sb("p_index_f", [P, 1])
        tile_index = sb("tile_index", [P, NT], I32)
        iota_i = sb("iota_i", [P, P], I32)
        zero_rows = sb("zero_rows", [P, D])
        xe = sb("xe", [P, NB, D])
        xe_t = sb("xe_t", [P, 2, EB, P])
        silu = sb("silu", [P, 2, CH * P])
        gated = sb("gated", [P, 2, FB, CH * P])
        ye = sb("ye", [P, 2, EB, D])

        x_loaded = sem("x_loaded")
        w_loaded = sem("w_loaded")
        small_loaded = sem("small_loaded")
        shared_loaded = sem("shared_loaded")
        experts_loaded = sem("experts_loaded")
        ctx_loaded = [sem("ctx_loaded0"), sem("ctx_loaded1")]
        pool_consts = sem("pool_consts")
        pool_step = sem("pool_step")
        dve_step = sem("dve_step")
        mask_ready = sem("mask_ready")
        w_transposed = sem("w_transposed")
        w_ready = sem("w_ready")
        xn_ready = sem("xn_ready")
        xc_transposed = sem("xc_transposed")
        xc_ready = sem("xc_ready")
        qk_projected = sem("qk_projected")
        qk_high = sem("qk_high")
        qk_low = sem("qk_low")
        qk_masked = sem("qk_masked")
        v_projected = sem("v_projected")
        v_placed = sem("v_placed")
        scored = sem("scored")
        max_ready = sem("max_ready")
        shift_ready = sem("shift_ready")
        exp_ready = sem("exp_ready")
        p_transposed = sem("p_transposed")
        p_copied = sem("p_copied")
        att_summed = sem("att_summed")
        att_step = sem("att_step")
        att_ready = sem("att_ready")
        att_transposed = sem("att_transposed")
        att_copied = sem("att_copied")
        att_projected = sem("att_projected")
        x1_ready = sem("x1_ready")
        stats_ready = sem("stats_ready")
        x1_kept = sem("x1_kept")
        t_ready = sem("t_ready")
        t_stored = [sem("t_stored0"), sem("t_stored1")]
        t_transposed = sem("t_transposed")
        h_ready = sem("h_ready")
        h_kept = sem("h_kept")
        routed = sem("routed")
        logits_ready = sem("logits_ready")
        gate_exp_in = sem("gate_exp_in")
        gate_exp = sem("gate_exp")
        onehot_ready = sem("onehot_ready")
        counted = sem("counted")
        carried_ready = sem("carried_ready")
        tabled = sem("tabled")
        table_ready = sem("table_ready")
        gathered = [sem(f"gathered{e}") for e in range(E)]
        up_done = sem("up_done")
        silu_ready = sem("silu_ready")
        gated_ready = sem("gated_ready")
        down_done = sem("down_done")
        summed = sem("summed")
        zero_ready = sem("zero_ready")
        out_stored = sem("out_stored")
        xe_transposed = sem("xe_transposed")
        xe_ready = sem("xe_ready")
        scattered = sem("scattered")

        block = stack.enter_context(nc.Block())

        FIRST, LAST = -2, NT + 2
        LOOP_FROM, LOOP_TO = 4, NT - 2

        def pipeline(engine, step):
            for i in range(FIRST, LOOP_FROM):
                step(i, i % 2)
            with engine.Fori(LOOP_FROM // 2, LOOP_TO // 2, 1) as pair:
                step(pair * 2, 0)
                step(pair * 2 + 1, 1)
            for i in range(LOOP_TO, LAST):
                step(i, i % 2)

        def live(n):
            return not isinstance(n, int) or 0 <= n < NT

        @block.sync
        def _(sp):
            q = NT // 4
            for n, w in enumerate((wq, wk, wv, wo)):
                sp.dma_start(w_raw[:, n, :], w).then_inc(w_loaded, 16)
            sp.dma_start(x_sb[:, 0:q, :], x_tiles[:, 0:q, :]).then_inc(x_loaded, 16)
            for n in range(2):
                sp.dma_start(ctx_sb[:, n, :], ctx_rows[n * P:(n + 1) * P, :]).then_inc(ctx_loaded[n], 16)
                sp.dma_start(mask_u8[n * S:(n + 1) * S, :], mask).then_inc(small_loaded, 16)
            for n in range(1, 4):
                sp.dma_start(x_sb[:, n * q:(n + 1) * q, :], x_tiles[:, n * q:(n + 1) * q, :]).then_inc(x_loaded, 16)
            sp.dma_start(g_col[:, :], ln_g.rearrange("(p a) -> p a", a=1)).then_inc(small_loaded, 16)
            sp.dma_start(b_col[:, :], ln_b.rearrange("(p a) -> p a", a=1)).then_inc(small_loaded, 16)
            sp.dma_start(wr_sb[:, :], wr).then_inc(small_loaded, 16)
            sp.dma_start(w1_sb[:, E, :], w1s).then_inc(shared_loaded, 16)
            sp.dma_start(w3_sb[:, E, :], w3s).then_inc(shared_loaded, 16)
            sp.dma_start(w2_sb[:, E, :, :], w2s.rearrange("(f p) d -> p f d", p=P)).then_inc(shared_loaded, 16)

            def step(i, par):
                n = i + 3
                if live(n) and live(n - 2):
                    at_least(sp, xc_transposed, n - 1)
                    sp.dma_start(ctx_sb[:, (par + 1) % 2, :], ctx_rows[bass.ds(n * P, P), :])\
                      .then_inc(ctx_loaded[(par + 1) % 2], 16)

            for i in range(FIRST, LOOP_FROM):
                step(i, i % 2)
            with sp.Fori(LOOP_FROM // 2, LOOP_TO // 2 - 1, 1) as pair:
                step(pair * 2, 0)
                step(pair * 2 + 1, 1)
            for i in range(LOOP_TO - 2, LAST):
                step(i, i % 2)
            for e in range(E):
                sp.dma_start(w1_sb[:, e, :], w1[e]).then_inc(experts_loaded, 16)
                sp.dma_start(w3_sb[:, e, :], w3[e]).then_inc(experts_loaded, 16)
                sp.dma_start(w2_sb[:, e, :, :], w2[e].rearrange("(f p) d -> p f d", p=P)).then_inc(experts_loaded, 16)
            with sp.Fori(0, NC // 2, 1) as pair:
                n = pair * 2
                for par in range(2):
                    sp.wait_ge(t_ready, n + (par + 1))
                    sp.dma_start(normed_tiles[:, bass.ds((n + par) * CH, CH), :], t_sb[:, par, :, :])\
                      .then_inc(t_stored[par], 16)
            sp.wait_ge(zero_ready, 1)
            sp.dma_start(out[T:T + P, :], zero_rows[:, :]).then_inc(out_stored, 16)
            with sp.Fori(0, NC, 1) as c:
                sp.wait_ge(summed, c + 1)
                sp.dma_start(out_tiles[:, bass.ds(c * CH, CH), :], x_sb[:, bass.ds(c * CH, CH), :]).then_inc(out_stored, 16)
            sp.wait_ge(scattered, 16 * EB * E)

        @block.gpsimd
        def _(pool):
            def const(ins):
                ins.then_inc(pool_step, 1)

            const(pool.memset(ident[:, :], 0.0))
            const(pool.memset(v_block[:], 0.0))
            const(pool.memset(group_mask[:], 0.0))
            const(pool.memset(upto[:, :], 1.0))
            const(pool.memset(mask_bias[:, :], 0.0))
            pool.wait_ge(pool_step, 5)
            pool.affine_select(out=ident[:, :], in_=ident[:, :], compare_op=ALU.not_equal, fill=1.0, base=0,
                               pattern=[[-1, P]], channel_multiplier=1).then_inc(pool_consts, 1)
            done = [1]

            def apart(ins):
                done[0] += 1
                ins.then_inc(pool_consts, 1)
                pool.wait_ge(pool_consts, done[0])

            pool.wait_ge(pool_consts, 1)
            for half in range(2):
                for par in range(2):
                    for b in range(2):
                        apart(pool.memset(v_block[half * S:(half + 1) * S, par, b, :, half, HD:HD + 1], 1.0))
            for g in range(G):
                apart(pool.memset(group_mask[g * 32:(g + 1) * 32, g, :], 1.0))
            pool.affine_select(out=upto[:, :], in_=upto[:, :], compare_op=ALU.is_ge, fill=0.0, base=0,
                               pattern=[[1, P]], channel_multiplier=-1).then_inc(pool_consts, 1)
            pool.iota(j_index[:], pattern=[[1, J], [0, P]], base=0, channel_multiplier=0).then_inc(pool_consts, 1)
            pool.iota(p_index[:, :], pattern=[[0, 1]], base=0, channel_multiplier=1).then_inc(pool_consts, 1)
            pool.iota(iota_i[:, :], pattern=[[1, P]], base=0, channel_multiplier=0).then_inc(pool_consts, 1)
            pool.iota(tile_index[:, :], pattern=[[1, NT]], base=1, channel_multiplier=0).then_inc(pool_consts, 1)
            pool.memset(ones_b[:, :], 1.0).then_inc(pool_consts, 1)
            pool.memset(zeros[:, :], 0.0).then_inc(pool_consts, 1)
            pool.memset(zero_rows[:, :], 0.0).then_inc(zero_ready, 1)

            def keep_tile(n, par):
                at_least(pool, stats_ready, n + 1)
                pool.tensor_copy(x_sb[:, bass.ds(n, 1), :].rearrange("p a d -> p (a d)"), x1_now[:, par, :])
                pool.tensor_copy(stats_all[:, bass.ds(n, 1), :].rearrange("p a d -> p (a d)"), stats_now[:, par, :])\
                    .then_inc(x1_kept, 1)

            with pool.Fori(0, NT // 2, 1) as pair:
                keep_tile(pair * 2, 0)
                keep_tile(pair * 2 + 1, 1)

            pool.wait_ge(table_ready, 1)
            for par in range(2):
                pool.wait_ge(t_stored[par], 16 * (NC // 2))
            for e in range(E):
                for k in range(EB):
                    s = e * EB + k
                    pool.indirect_dma_start(xe[:, s, :], None, normed,
                                            bass.IndirectOffsetOnAxis(ap=from_row[:, s:s + 1].bitcast(U32), axis=0))\
                        .then_inc(gathered[e], 16)
            pool.wait_ge(out_stored, 16 * (NC + 1))
            for e in range(E):
                at_least(pool, scattered, 16 * EB * e)
                pool.wait_ge(summed, NC + e + 1)
                for k in range(EB):
                    s = e * EB + k
                    pool.indirect_dma_start(out, bass.IndirectOffsetOnAxis(ap=to_row[:, s:s + 1].bitcast(U32), axis=0),
                                            ye[:, e % 2, k, :], None, compute_op=ALU.add).then_inc(scattered, 16)

        POOL_CONSTS = 1 + 8 + G + 1 + 4 + 2

        @block.tensor
        def _(pe):
            pe.wait_ge(pool_consts, 1)
            pe.wait_ge(w_loaded, 64)
            for n in range(4):
                ins = pe.transpose(bank[0][:, n * P:(n + 1) * P], w_raw[:, n, :], ident[:, :])
            ins.then_inc(w_transposed, 1)
            pe.wait_ge(pool_consts, POOL_CONSTS)
            pe.wait_ge(mask_ready, 1)
            pe.wait_ge(w_ready, 1)

            def transpose_inputs(n, par):
                pe.wait_ge(ctx_loaded[par], (n // 2 + 1) * 16 if isinstance(n, int) else (n - par) * 8 + 16)
                at_least(pe, xn_ready, n + 1)
                at_least(pe, qk_low, n)
                pe.transpose(bank[2][:, 0:P], xn[:, par, :], ident[:, :])
                pe.transpose(bank[2][:, P:2 * P], ctx_sb[:, par, :], ident[:, :]).then_inc(xc_transposed, 1)

            def project_qk(n):
                at_least(pe, xc_ready, n + 1)
                pe.matmul(bank[2][:, 2 * P:3 * P], w_t[:, 0, :], xc_t[:, 0, :], start=True, stop=True)
                pe.matmul(bank[2][:, 3 * P:4 * P], w_t[:, 1, :], xc_t[:, 1, :], start=True, stop=True)\
                  .then_inc(qk_projected, 1)

            def project_v(n):
                at_least(pe, v_placed, n * 2)
                for b in range(2):
                    for half in range(2):
                        ins = pe.matmul(bank[3][half * S:(half + 1) * S, b * P:(b + 1) * P],
                                        xc_t[:, 1, b * S:(b + 1) * S], w_t[:, 2, :], start=True, stop=True)
                ins.then_inc(v_projected, 1)

            def score(n, par, half):
                at_least(pe, qk_masked, n + 1)
                at_least(pe, shift_ready, n * 2 + (half - 1))
                for b in range(2):
                    pe.matmul(bank[half][b * S:(b + 1) * S, :], q_select[:, :],
                              mask_bias[:, :].unsqueeze(1).to_broadcast([P, HH, S]), start=True, stop=False)
                for gl in range(2):
                    for m, (qp, kp) in enumerate(((0, 0), (0, 1), (1, 0))):
                        for b in range(2):
                            ins = pe.matmul(bank[half][b * S:(b + 1) * S, gl * J * S:(gl + 1) * J * S],
                                            q_masked[:, par, qp, half * 2 + gl, b * S:(b + 1) * S],
                                            k_masked[:, par, kp, :, b * S:(b + 1) * S],
                                            start=False, stop=(gl == 1 and m == 2))
                ins.then_inc(scored, 1)

            def transpose_probs(n, par, half):
                at_least(pe, exp_ready, n * 2 + (half + 1))
                at_least(pe, p_copied, n * 2 + (half - 1))
                for c in range(HH // 2):
                    ins = pe.transpose(bank[4 + half][:, c * P:(c + 1) * P],
                                       probs[:, par, half, c * P:(c + 1) * P], ident[:, :])
                ins.then_inc(p_transposed, 1)

            def weigh_values(n, par):
                at_least(pe, p_copied, n * 2 + 2)
                at_least(pe, v_placed, n * 2 + 2)
                at_least(pe, att_ready, n)
                for pair in range(H // 2):
                    for b in range(2):
                        W = 2 * (HD + 1)
                        ins = pe.matmul(bank[6][b * S:(b + 1) * S, pair * W:(pair + 1) * W],
                                        probs_t[:, pair // (HH // 2), pair % (HH // 2), b * S:(b + 1) * S],
                                        v_block[:, par, b, pair, :, :].rearrange("p a d -> p (a d)"),
                                        start=True, stop=True)
                ins.then_inc(att_summed, 1)

            def transpose_att(n):
                at_least(pe, att_ready, n + 1)
                at_least(pe, x1_ready, n)
                pe.transpose(bank[7][:, 0:P], att[:, :, :].rearrange("p h d -> p (h d)"), ident[:, :])\
                  .then_inc(att_transposed, 1)

            def project_out(n):
                at_least(pe, att_copied, n + 1)
                pe.matmul(bank[7][:, P:2 * P], att_t[:, :], w_t[:, 3, :], start=True, stop=True)\
                  .then_inc(att_projected, 1)

            def step(i, par):
                if live(i + 1):
                    transpose_inputs(i + 1, 1 - par)
                if live(i):
                    score(i, par, 0)
                if live(i - 2):
                    transpose_att(i - 2)
                if live(i - 1):
                    transpose_probs(i - 1, 1 - par, 0)
                if live(i + 1):
                    project_qk(i + 1)
                if live(i):
                    score(i, par, 1)
                if live(i - 2):
                    project_out(i - 2)
                if live(i - 1):
                    transpose_probs(i - 1, 1 - par, 1)
                    weigh_values(i - 1, 1 - par)
                if live(i + 1):
                    project_v(i + 1)

            pipeline(pe, step)

            def to_hidden(c, par):
                pe.wait_ge(t_ready, c + 1)
                at_least(pe, h_kept, c - 1)
                for k in range(CH):
                    ins = pe.transpose(bank[par][:, k * P:(k + 1) * P], t_sb[:, par, k, :], ident[:, :])
                ins.then_inc(t_transposed, 1)

            def route(c, par):
                pe.wait_ge(h_ready, c + 1)
                at_least(pe, logits_ready, c - 1)
                for k in range(CH):
                    ins = pe.matmul(bank[2 + par][:, k * E:(k + 1) * E], h_now[:, par, k * P:(k + 1) * P], wr_sb[:, :],
                                    start=True, stop=True)
                ins.then_inc(routed, 1)

            to_hidden(0, 0)
            to_hidden(1, 1)
            for par in range(2):
                route(par, par)
                to_hidden(par + 2, par)
            with pe.Fori(1, NC // 2 - 1, 1) as pair:
                c = pair * 2
                for par in range(2):
                    route(c + par, par)
                    to_hidden(c + (par + 2), par)
            route(NC - 2, 0)
            route(NC - 1, 1)

            def count_choices():
                pe.wait_ge(onehot_ready, 1)
                flat = one_hot_b[:, :, :].rearrange("p c e -> p (c e)")
                pe.matmul(bank[6][:, 0:CT * E], upto[:, :], flat, start=True, stop=True)
                pe.matmul(bank[7][:, 0:CT * E], ones_b[:, :], flat, start=True, stop=True).then_inc(counted, 1)

            def fill_table():
                for ct in range(CT):
                    if ct % LC == 0:
                        pe.wait_ge(carried_ready, ct // LC + 1)
                    half = ct // LC % 2
                    ins = pe.matmul(bank[6][:, 0:VALS * NB], at_lane[:, half, ct % LC, :],
                                    carried[:, half, ct % LC, :, :].rearrange("p v n -> p (v n)"),
                                    start=(ct == 0), stop=(ct == CT - 1))
                    if ct % LC == LC - 1:
                        ins.then_inc(tabled, 1)

            def up(n, f, e, rhs):
                at_least(pe, gated_ready, n * FB + (f - 1))
                a, width = 2 * (f % 2), rhs.shape[1]
                pe.matmul(bank[a][:, 0:width], w1_sb[:, e, f * P:(f + 1) * P], rhs, start=True, stop=True)
                pe.matmul(bank[a + 1][:, 0:width], w3_sb[:, e, f * P:(f + 1) * P], rhs, start=True, stop=True)\
                  .then_inc(up_done, 1)

            def down(n, par, e, tiles):
                pe.wait_ge(gated_ready, n * FB + FB)
                at_least(pe, summed, n - 1)
                for k in range(tiles):
                    for f in range(FB):
                        ins = pe.matmul(bank[4 + par][:, k * P:(k + 1) * P], gated[:, par, f, k * P:(k + 1) * P],
                                        w2_sb[:, e, f, :], start=(f == 0), stop=(f == FB - 1))
                ins.then_inc(down_done, 1)

            def shared_unit(n, par, first=False):
                rhs = h_t[:, bass.ds(n * CH * P, CH * P)]
                up(n, 0, E, rhs)
                up(n, 1, E, rhs)
                if not first:
                    down(n - 1, 1 - par, E, CH)
                up(n, 2, E, rhs)
                up(n, 3, E, rhs)

            pe.wait_ge(shared_loaded, 48)
            pe.wait_ge(h_kept, NC)
            count_choices()
            shared_unit(0, 0, first=True)
            shared_unit(1, 1)
            shared_unit(2, 0)
            fill_table()
            shared_unit(3, 1)
            with pe.Fori(2, NC // 2, 1) as pair:
                n = pair * 2
                shared_unit(n, 0)
                shared_unit(n + 1, 1)

            def transpose_slots(e):
                pe.wait_ge(gathered[e], 16 * EB)
                at_least(pe, xe_ready, e)
                for k in range(EB):
                    ins = pe.transpose(bank[7][:, k * P:(k + 1) * P], xe[:, e * EB + k, :], ident[:, :])
                ins.then_inc(xe_transposed, 1)

            pe.wait_ge(experts_loaded, 48 * E)
            transpose_slots(0)
            for e in range(E):
                n = NC + e
                pe.wait_ge(xe_ready, e + 1)
                rhs = xe_t[:, e % 2, :, :].rearrange("p k n -> p (k n)")
                up(n, 0, e, rhs)
                up(n, 1, e, rhs)
                down(n - 1, (n - 1) % 2, e - 1 if e else E, EB if e else CH)
                up(n, 2, e, rhs)
                up(n, 3, e, rhs)
                if e + 1 < E:
                    transpose_slots(e + 1)
            down(NC + E - 1, (NC + E - 1) % 2, E - 1, EB)

        @block.scalar
        def _(act):
            act.wait_ge(w_transposed, 1)
            act.activation(w_t[:, :, :], bank[0][:, :].rearrange("p (n m) -> p n m", n=4), ACT.Copy).then_inc(w_ready, 1)

            def copy_inputs(n):
                at_least(act, xc_transposed, n + 1)
                act.activation(xc_t[:, :, :], bank[2][:, 0:2 * P].rearrange("p (a n) -> p a n", a=2), ACT.Copy)\
                   .then_inc(xc_ready, 1)

            def copy_att(n):
                at_least(act, att_transposed, n + 1)
                act.activation(att_t[:, :], bank[7][:, 0:P], ACT.Copy).then_inc(att_copied, 1)

            def copy_probs(n, half):
                at_least(act, p_transposed, n * 2 + (half + 1))
                at_least(act, att_summed, n)
                act.activation(probs_t[:, half, :, :], bank[4 + half][:, :].rearrange("p (c n) -> p c n", n=P), ACT.Copy)\
                   .then_inc(p_copied, 1)

            def high_parts(n):
                at_least(act, qk_projected, n + 1)
                at_least(act, qk_masked, n)
                act.activation(qk_parts[:, 0, :, :], bank[2][:, 2 * P:4 * P].rearrange("p (a n) -> p a n", a=2), ACT.Copy)\
                   .then_inc(qk_high, 1)

            def exponentials(n, par, half):
                at_least(act, shift_ready, n * 2 + (half + 1))
                act.activation(probs[:, par, half, :], shifted[:, half, :, :].rearrange("p h k -> p (h k)"), ACT.Exp,
                               scale=SCALE).then_inc(exp_ready, 1)

            def place_values(n, par):
                at_least(act, v_projected, n + 1)
                for half in range(2):
                    rows = slice(half * S, (half + 1) * S)
                    ins = act.activation(
                        v_block[rows, par, :, :, half, 0:HD].rearrange("p b h d -> p (b h) d"),
                        bank[3][rows, 0:2 * P].rearrange("p (h a d) -> p h a d", a=2, d=HD)[:, :, half, :], ACT.Copy)
                    ins.then_inc(v_placed, 1)

            def step(i, par):
                if live(i + 1):
                    copy_inputs(i + 1)
                if live(i - 2):
                    copy_att(i - 2)
                if live(i - 1):
                    copy_probs(i - 1, 0)
                if live(i + 1):
                    high_parts(i + 1)
                if live(i):
                    exponentials(i, par, 0)
                if live(i - 1):
                    copy_probs(i - 1, 1)
                if live(i + 1):
                    place_values(i + 1, 1 - par)
                if live(i):
                    exponentials(i, par, 1)

            pipeline(act, step)

            act.wait_ge(pool_consts, POOL_CONSTS)
            with act.Fori(0, NC // 2, 1) as pair:
                c = pair * 2
                for par in range(2):
                    act.wait_ge(h_ready, c + (par + 1))
                    act.activation(h_t[:, bass.ds((c + par) * CH * P, CH * P)], bank[par][:, :], ACT.Identity,
                                   scale=g_col[:, :], bias=b_col[:, :]).then_inc(h_kept, 1)
            act.wait_ge(gate_exp_in, 1)
            act.activation(gate_e[:, :], gate_d[:, :], ACT.Exp).then_inc(gate_exp, 1)

            def silu_unit(n, width):
                for f in range(FB):
                    act.wait_ge(up_done, n * FB + (f + 1))
                    at_least(act, gated_ready, n * FB + (f - 1))
                    act.activation(silu[:, f % 2, 0:width], bank[2 * (f % 2)][:, 0:width], ACT.Silu)\
                       .then_inc(silu_ready, 1)

            for n in range(2):
                silu_unit(n, CH * P)
            with act.Fori(2, NC, 1) as n:
                silu_unit(n, CH * P)
            for e in range(E):
                silu_unit(NC + e, EB * P)

        @block.vector
        def _(dve):
            chain = Chain(dve, dve_step)
            then = chain.then

            def inverse_root(out_, v, scratch):
                then(dve.tensor_scalar(out_.bitcast(I32), v.bitcast(I32), 1, None, ALU.logical_shift_right))
                then(dve.tensor_scalar(out_.bitcast(I32), out_.bitcast(I32), -1.0, float(0x5f3759df), ALU.mult, ALU.add))
                for _ in range(3):
                    then(dve.tensor_tensor(scratch, out_, out_, ALU.mult))
                    then(dve.tensor_tensor(scratch, scratch, v, ALU.mult))
                    then(dve.tensor_scalar(scratch, scratch, -0.5, 1.5, ALU.mult, ALU.add))
                    then(dve.tensor_tensor(out_, out_, scratch, ALU.mult))

            dve.wait_ge(pool_step, 5)
            dve.wait_ge(small_loaded, 16 * 5)
            then(dve.tensor_scalar(mask_bias[0:S, :], mask_u8[0:S, :], -1.0, 1e9 / SCALE, ALU.add, ALU.mult))
            then(dve.tensor_reduce(row_any[:, :], mask_u8[:, :], X, ALU.max))
            dve.wait_ge(pool_consts, POOL_CONSTS)
            then(dve.tensor_copy(q_select[:, :], ident[:, 0:S]))
            then(dve.tensor_scalar(p_head[:, :], p_index[:, :], 3, J - 1, ALU.logical_shift_right, ALU.bitwise_and))
            then(dve.tensor_copy(p_head_f[:, :], p_head[:, :]))
            dve.tensor_scalar(slot_mask[:, :, :], j_index[:, :, :], p_head_f[:, 0:1], None, ALU.is_equal)\
               .then_inc(mask_ready, 1)
            dve.wait_ge(mask_ready, 1)
            for n in range(NT):
                if n % (NT // 4) == 0:
                    dve.wait_ge(x_loaded, 16 * 4)
                then(dve.bn_stats(stats[:, :], x_sb[:, n, :]))
                then(dve.bn_aggr(moments[:, n, :], stats[:, :]))
            then(dve.tensor_scalar(variance[:, :], moments[:, :, 1], EPS, None, ALU.add))
            inverse_root(rstd[:, :], variance[:, :], newton[:, :])

            def normalise(n, par):
                at_least(dve, xc_transposed, n - 1)
                dve.tensor_scalar(xn[:, par, :], x_sb[:, bass.ds(n, 1), :].rearrange("p a d -> p (a d)"),
                                  moments[:, bass.ds(n, 1), 0:1].rearrange("p a b -> p (a b)"),
                                  rstd[:, bass.ds(n, 1)], ALU.subtract, ALU.mult).then_inc(xn_ready, 1)

            def shift_by_max(n, half):
                at_least(dve, scored, n * 2 + (half + 1))
                scores = bank[half][:, :].rearrange("p (h k) -> p h k", k=S)
                dve.tensor_reduce(row_max[:, half, :], scores, X, ALU.max).then_inc(max_ready, 1)
                at_least(dve, max_ready, n * 2 + (half + 1))
                at_least(dve, exp_ready, n * 2 + (half - 1))
                dve.tensor_tensor(shifted[:, half, :, :], scores,
                                  row_max[:, half, :].unsqueeze(2).to_broadcast([P, HH, S]), ALU.subtract)\
                   .then_inc(shift_ready, 1)

            def spread_qk(n, par):
                at_least(dve, qk_high, n + 1)
                dve.tensor_tensor(qk_parts[:, 1, :, :], bank[2][:, 2 * P:4 * P].rearrange("p (a n) -> p a n", a=2),
                                  qk_parts[:, 0, :, :], ALU.subtract).then_inc(qk_low, 1)
                at_least(dve, qk_low, n + 1)
                dve.tensor_tensor(q_masked[:, par, :, :, :],
                                  qk_parts[:, :, 0, :].unsqueeze(2).to_broadcast([P, 2, G, P]),
                                  group_mask[:, :, :].unsqueeze(1).to_broadcast([P, 2, G, P]), ALU.mult)
                dve.tensor_tensor(k_masked[:, par, :, :, :],
                                  qk_parts[:, :, 1, :].unsqueeze(2).to_broadcast([P, 2, J, P]),
                                  slot_mask[:, :, :].unsqueeze(1).to_broadcast([P, 2, J, P]), ALU.mult)\
                   .then_inc(qk_masked, 1)

            def divide_by_sum(n):
                at_least(dve, att_summed, n + 1)
                sums = bank[6][:, 0:H * (HD + 1)].rearrange("p (h d) -> p h d", d=HD + 1)
                dve.tensor_scalar(att_sum[:, :], sums[:, :, HD], 1e-9, None, ALU.max).then_inc(att_step, 1)
                dve.wait_ge(att_step, n * 2 + 1)
                dve.reciprocal(att_inv[:, :], att_sum[:, :]).then_inc(att_step, 1)
                dve.wait_ge(att_step, n * 2 + 2)
                dve.scalar_tensor_tensor(out=att[:, :, :], in0=sums[:, :, 0:HD], scalar=row_any[:, 0:1],
                                         in1=att_inv[:, :].unsqueeze(2).to_broadcast([P, H, HD]),
                                         op0=ALU.mult, op1=ALU.mult).then_inc(att_ready, 1)

            def add_residual(n, par):
                at_least(dve, att_projected, n + 1)
                at_least(dve, x1_kept, n - 1)
                dve.tensor_tensor(x1_now[:, par, :], x_sb[:, bass.ds(n, 1), :].rearrange("p a d -> p (a d)"),
                                  bank[7][:, P:2 * P], ALU.add).then_inc(x1_ready, 1)
                at_least(dve, x1_ready, n + 1)
                dve.bn_stats(stats_now[:, par, :], x1_now[:, par, :]).then_inc(stats_ready, 1)

            def step(i, par):
                if live(i + 2):
                    normalise(i + 2, par)
                if live(i):
                    shift_by_max(i, 0)
                if live(i + 1):
                    spread_qk(i + 1, 1 - par)
                if live(i - 2):
                    add_residual(i - 2, par)
                if live(i):
                    shift_by_max(i, 1)
                if live(i - 1):
                    divide_by_sum(i - 1)

            pipeline(dve, step)

            dve.wait_ge(x1_kept, NT)
            even, odd = stats_all[:, :, 1], stats_all[:, :, 4]
            then(dve.tensor_tensor(variance[:, :], stats_all[:, :, 2], stats_all[:, :, 5], ALU.add))
            then(dve.tensor_tensor(newton[:, :], even, odd, ALU.subtract))
            then(dve.tensor_tensor(newton[:, :], newton[:, :], newton[:, :], ALU.mult))
            then(dve.scalar_tensor_tensor(out=variance[:, :], in0=newton[:, :], scalar=D / 4.0, in1=variance[:, :],
                                          op0=ALU.mult, op1=ALU.add))
            then(dve.tensor_scalar(moments[:, :, 1], variance[:, :], 1.0 / D, None, ALU.mult))
            then(dve.tensor_tensor(newton[:, :], even, odd, ALU.add))
            then(dve.tensor_scalar(moments[:, :, 0], newton[:, :], 0.5, None, ALU.mult))
            then(dve.tensor_scalar(variance[:, :], moments[:, :, 1], 1.0 + EPS, EPS * EPS, ALU.mult, ALU.add))
            inverse_root(rstd[:, :], variance[:, :], newton[:, :])

            def normalise_chunk(c, par):
                at_least(dve, t_transposed, c - 1)
                at_least(dve, t_stored[par], (c // 2) * 16 if isinstance(c, int) else (c - par) * 8)
                for k in range(CH):
                    ins = dve.tensor_scalar(t_sb[:, par, k, :],
                                            x_sb[:, bass.ds(c * CH + k, 1), :].rearrange("p a d -> p (a d)"),
                                            moments[:, bass.ds(c * CH + k, 1), 0:1].rearrange("p a b -> p (a b)"),
                                            rstd[:, bass.ds(c * CH + k, 1)], ALU.subtract, ALU.mult)
                ins.then_inc(t_ready, 1)

            def scale_chunk(c, par):
                at_least(dve, t_transposed, c + 1)
                at_least(dve, routed, c - 1)
                dve.tensor_scalar(h_now[:, par, :], bank[par][:, :], g_col[:, 0:1], b_col[:, 0:1], ALU.mult, ALU.add)\
                   .then_inc(h_ready, 1)

            def keep_logits(c, par):
                at_least(dve, routed, c + 1)
                dve.tensor_copy(logits[:, bass.ds(c * CH, CH), :],
                                bank[2 + par][:, 0:CH * E].rearrange("p (k e) -> p k e", k=CH)).then_inc(logits_ready, 1)

            normalise_chunk(0, 0)
            normalise_chunk(1, 1)
            scale_chunk(0, 0)
            scale_chunk(1, 1)
            with dve.Fori(1, NC // 2, 1) as pair:
                c = pair * 2
                for par in range(2):
                    normalise_chunk(c + par, par)
                    keep_logits(c + (par - 2), par)
                    scale_chunk(c + par, par)
            keep_logits(NC - 2, 0)
            keep_logits(NC - 1, 1)
            dve.wait_ge(logits_ready, NC)

            then(dve.tensor_copy(e_index[:, :], iota_i[:, 0:E]))
            then(dve.tensor_scalar(by_index[:, :], e_index[:, :], -1.0, float(E), ALU.mult, ALU.add))
            spread = [P, NT, E]
            source = logits
            for c in range(TOP_K):
                if c:
                    then(dve.scalar_tensor_tensor(out=rest[:, :, :], in0=one_hot[:, 0:NT, :], scalar=-3e38,
                                                  in1=logits[:, :, :], op0=ALU.mult, op1=ALU.add))
                    source = rest
                then(dve.tensor_reduce(top[:, c, :], source[:, :, :], X, ALU.max))
                then(dve.tensor_tensor(eq[:, :, :], source[:, :, :], top[:, c, :].unsqueeze(2).to_broadcast(spread),
                                       ALU.is_equal))
                then(dve.tensor_tensor(eq[:, :, :], eq[:, :, :], by_index[:, :].unsqueeze(1).to_broadcast(spread), ALU.mult))
                then(dve.tensor_reduce(pick[:, :], eq[:, :, :], X, ALU.max))
                then(dve.tensor_tensor(one_hot[:, c * NT:(c + 1) * NT, :], eq[:, :, :],
                                       pick[:, :].unsqueeze(2).to_broadcast(spread), ALU.is_equal))
            dve.tensor_copy(one_hot_b[:, :, :], one_hot[:, :, :]).then_inc(onehot_ready, 1)
            dve.tensor_tensor(gate_d[:, :], top[:, 1, :], top[:, 0, :], ALU.subtract).then_inc(gate_exp_in, 1)

            def rank_choices():
                dve.wait_ge(counted, 1)
                then(dve.tensor_copy(totals[:, :, :], bank[7][:, 0:CT * E].rearrange("p (c e) -> p c e", e=E)))
                for e in range(E):
                    then(dve.tensor_tensor_scan(running[:, :, e], totals[:, :, e], zeros[:, :], 0.0, ALU.add, ALU.add))
                then(dve.tensor_tensor(running[:, :, :], running[:, :, :], totals[:, :, :], ALU.subtract))
                then(dve.tensor_tensor(place[:, :, :], bank[6][:, 0:CT * E].rearrange("p (c e) -> p c e", e=E),
                                       running[:, :, :], ALU.add))
                then(dve.tensor_tensor(place[:, :, :], place[:, :, :], one_hot[:, :, :], ALU.mult))
                then(dve.tensor_reduce(rank[:, :], place[:, :, :], X, ALU.add))
                then(dve.tensor_tensor(running[:, :, :], one_hot[:, :, :],
                                       e_index[:, :].unsqueeze(1).to_broadcast([P, CT, E]), ALU.mult))
                then(dve.tensor_reduce(expert[:, :], running[:, :, :], X, ALU.add))
                then(dve.tensor_scalar(keep[:, :], rank[:, :], float(CAP), None, ALU.is_le))
                then(dve.tensor_scalar(past1[:, :], rank[:, :], float(P), None, ALU.is_gt))
                for k in range(2, EB):
                    then(dve.scalar_tensor_tensor(out=past1[:, :], in0=rank[:, :], scalar=float(k * P),
                                                  in1=past1[:, :], op0=ALU.is_gt, op1=ALU.add))
                then(dve.scalar_tensor_tensor(out=blk_b[:, :], in0=expert[:, :], scalar=float(EB), in1=past1[:, :],
                                              op0=ALU.mult, op1=ALU.add))
                then(dve.scalar_tensor_tensor(out=lo[:, :], in0=past1[:, :], scalar=-float(P), in1=rank[:, :],
                                              op0=ALU.mult, op1=ALU.add))
                then(dve.tensor_tensor(lo[:, :], lo[:, :], keep[:, :], ALU.mult))
                then(dve.tensor_scalar(lo_b[:, :], lo[:, :], -1.0, None, ALU.add))
                dve.wait_ge(gate_exp, 1)
                then(dve.tensor_scalar(gate_d[:, :], gate_e[:, :], 1.0, None, ALU.add))
                then(dve.reciprocal(gates[:, 0, :], gate_d[:, :]))
                then(dve.tensor_tensor(gates[:, 1, :], gate_e[:, :], gates[:, 0, :], ALU.mult))
                flat = gates[:, :, :].rearrange("p c t -> p (c t)")
                then(dve.tensor_copy(vals[:, :, 2], flat))
                then(dve.tensor_tensor(gate_rest[:, :], flat, vals[:, :, 2], ALU.subtract))
                then(dve.tensor_copy(vals[:, :, 3], gate_rest[:, :]))
                then(dve.tensor_tensor(gate_rest[:, :], gate_rest[:, :], vals[:, :, 3], ALU.subtract))
                then(dve.tensor_copy(vals[:, :, 4], gate_rest[:, :]))
                for c in range(TOP_K):
                    then(dve.tensor_copy(vals[:, c * NT:(c + 1) * NT, 0], tile_index[:, :]))
                then(dve.tensor_copy(p_index_f[:, :], p_index[:, :]))
                then(dve.tensor_copy(vals[:, :, 1], p_index_f[:, 0:1].to_broadcast([P, CT])))
                then(dve.tensor_copy(lane[:, :], iota_i[:, :]))
                then(dve.tensor_copy(blocks[:, :], iota_i[:, 0:NB]))

            def carry_values(parts):
                for c in (part * LC for part in parts):
                    w, half = slice(c, c + LC), c // LC % 2
                    at_least(dve, tabled, c // LC - 1)
                    dve.tensor_tensor(at_lane[:, half, :, :], lane[:, :].unsqueeze(1).to_broadcast([P, LC, P]),
                                      lo_b[:, w].unsqueeze(2).to_broadcast([P, LC, P]), ALU.is_equal)
                    at_least(dve, carried_ready, c // LC)
                    then(dve.tensor_tensor(at_block[:, :, :], blocks[:, :].unsqueeze(1).to_broadcast([P, LC, NB]),
                                           blk_b[:, w].unsqueeze(2).to_broadcast([P, LC, NB]), ALU.is_equal))
                    dve.tensor_tensor(carried[:, half, :, :, :],
                                      at_block[:, :, :].unsqueeze(2).to_broadcast([P, LC, VALS, NB]),
                                      vals[:, w, :].unsqueeze(3).to_broadcast([P, LC, VALS, NB]), ALU.mult)\
                       .then_inc(carried_ready, 1)

            def read_table():
                dve.wait_ge(tabled, CT // LC)
                then(dve.tensor_copy(table[:, :, :], bank[6][:, 0:VALS * NB].rearrange("p (v n) -> p v n", v=VALS)))
                then(dve.tensor_scalar(used[:, :], table[:, 0, :], 0.5, None, ALU.is_gt))
                then(dve.scalar_tensor_tensor(out=token[:, :], in0=table[:, 0, :], scalar=float(P), in1=table[:, 1, :],
                                              op0=ALU.mult, op1=ALU.add))
                then(dve.tensor_scalar(token[:, :], token[:, :], -float(P), 0.0, ALU.add, ALU.max))
                then(dve.tensor_copy(from_row[:, :], token[:, :]))
                then(dve.tensor_scalar(spare[:, :], p_index_f[:, 0:1].to_broadcast([P, NB]), float(T), None, ALU.add))
                then(dve.tensor_tensor(token[:, :], token[:, :], spare[:, :], ALU.subtract))
                then(dve.tensor_tensor(token[:, :], token[:, :], used[:, :], ALU.mult))
                then(dve.tensor_tensor(to_row[:, :], token[:, :], spare[:, :], ALU.add))
                then(dve.tensor_tensor(slot_gate[:, :], table[:, 2, :], table[:, 3, :], ALU.add))
                dve.tensor_tensor(slot_gate[:, :], slot_gate[:, :], table[:, 4, :], ALU.add).then_inc(table_ready, 1)

            def gate_units(n, par, fs, width):
                for f in fs:
                    dve.wait_ge(silu_ready, n * FB + (f + 1))
                    at_least(dve, down_done, n - 1)
                    dve.tensor_tensor(gated[:, par, f, 0:width], silu[:, f % 2, 0:width],
                                      bank[2 * (f % 2) + 1][:, 0:width], ALU.mult).then_inc(gated_ready, 1)

            def add_shared(n, par):
                dve.wait_ge(down_done, n + 1)
                rows = x_sb[:, bass.ds(n * CH, CH), :]
                dve.tensor_tensor(rows, rows, bank[4 + par][:, :].rearrange("p (k d) -> p k d", k=CH), ALU.add)\
                   .then_inc(summed, 1)

            def shared_unit(n, par, first=False):
                gate_units(n, par, (0, 1), CH * P)
                if not first:
                    add_shared(n - 1, 1 - par)
                gate_units(n, par, (2, 3), CH * P)

            shared_unit(0, 0, first=True)
            rank_choices()
            shared_unit(1, 1)
            carry_values((0, 1))
            shared_unit(2, 0)
            carry_values((2, 3))
            shared_unit(3, 1)
            read_table()
            with dve.Fori(2, NC // 2, 1) as pair:
                n = pair * 2
                shared_unit(n, 0)
                shared_unit(n + 1, 1)

            def scale_slots(e):
                dve.wait_ge(xe_transposed, e + 1)
                dve.tensor_scalar(xe_t[:, e % 2, :, :], bank[7][:, 0:EB * P].rearrange("p (k n) -> p k n", k=EB),
                                  g_col[:, 0:1], b_col[:, 0:1], ALU.mult, ALU.add).then_inc(xe_ready, 1)

            def gate_outputs(e):
                n = NC + e
                dve.wait_ge(down_done, n + 1)
                at_least(dve, scattered, 16 * EB * (e - 1))
                for k in range(EB):
                    ins = dve.tensor_scalar(ye[:, e % 2, k, :], bank[4 + n % 2][:, k * P:(k + 1) * P],
                                            slot_gate[:, e * EB + k:e * EB + k + 1], None, ALU.mult)
                ins.then_inc(summed, 1)

            dve.wait_ge(table_ready, 1)
            scale_slots(0)
            for e in range(E):
                n = NC + e
                gate_units(n, n % 2, (0, 1), EB * P)
                if e:
                    gate_outputs(e - 1)
                else:
                    add_shared(NC - 1, (NC - 1) % 2)
                gate_units(n, n % 2, (2, 3), EB * P)
                if e + 1 < E:
                    scale_slots(e + 1)
            gate_outputs(E - 1)


def kernel(x, ctx_1024, mask_SxS2_bk0, L0_xattn_Wq, L0_xattn_Wk, L0_xattn_Wv, L0_xattn_Wo, L0_ffn_ln_g, L0_ffn_ln_b,
           L0_ffn_Wr, L0_ffn_W1, L0_ffn_W3, L0_ffn_W2, L0_ffn_W1s, L0_ffn_W3s, L0_ffn_W2s):
    import numpy as np
    import concourse.bacc as bacc
    from concourse.bass_utils import run_bass_kernel_spmd

    given = [x, ctx_1024, mask_SxS2_bk0, L0_xattn_Wq, L0_xattn_Wk, L0_xattn_Wv, L0_xattn_Wo, L0_ffn_ln_g, L0_ffn_ln_b,
             L0_ffn_Wr, L0_ffn_W1, L0_ffn_W3, L0_ffn_W2, L0_ffn_W1s, L0_ffn_W3s, L0_ffn_W2s]
    names = ["x", "ctx", "mask", "wq", "wk", "wv", "wo", "ln_g", "ln_b", "wr", "w1", "w3", "w2", "w1s", "w3s", "w2s"]
    nc = bacc.Bacc("TRN2", target_bir_lowering=False, num_devices=1)
    arrays, args = {}, []
    for name, a in zip(names, given):
        a = np.ascontiguousarray(a)
        arrays[f"in_{name}"] = a
        args.append(nc.dram_tensor(f"in_{name}", a.shape, mybir.dt.from_np(a.dtype), kind="ExternalInput").ap())
    B, S, D = x.shape
    normed = nc.dram_tensor("normed", (B * S, D), F32, kind="Internal").ap()
    out = nc.dram_tensor("out_rows", (B * S + P, D), F32, kind="ExternalOutput").ap()
    xattn_moe(nc, *args, normed, out)
    got = run_bass_kernel_spmd(nc, [arrays], core_ids=[0]).results[0]["out_rows"]
    return got[0:B * S].reshape(B, S, D)
```

```python
from contextlib import ExitStack

import concourse.bass as bass
from concourse import mybir

F32 = mybir.dt.float32
F32R = mybir.dt.float32r
F16 = mybir.dt.float16
BF16 = mybir.dt.bfloat16
I32 = mybir.dt.int32
U32 = mybir.dt.uint32
U8 = mybir.dt.uint8
ALU = mybir.AluOpType
ACT = mybir.ActivationFunctionType
X = mybir.AxisListType.X

P = 128
EPS = 1e-5
CAPACITY_TOKENS = 4 * 256
TOP_K = 2
BANKS = 8
BANK = 512


def at_least(engine, semaphore, value):
    if isinstance(value, int) and value <= 0:
        return
    engine.wait_ge(semaphore, value)


class Chain:

    def __init__(self, engine, semaphore):
        self.engine, self.semaphore, self.count = engine, semaphore, 0

    def then(self, instruction):
        self.count += 1
        instruction.then_inc(self.semaphore, 1)
        self.engine.wait_ge(self.semaphore, self.count)


def xattn_moe(nc, x, ctx, mask, wq, wk, wv, wo, ln_g, ln_b, wr, w1, w3, w2, w1s, w3s, w2s, normed, out):
    B, S, D = x.shape
    T = B * S
    NT = T // P
    H = 16
    HD = D // H
    SCALE = float(HD) ** -0.5
    E, _, F = w1.shape
    FB = F // P
    CAP = -(-5 * CAPACITY_TOKENS * TOP_K // (4 * E))
    EB = -(-CAP // P)
    NB = E * EB
    G = P // 32
    J = H // G
    HH = H // 2
    CH = 4
    NC = NT // CH
    assert S * 2 == P and D == P and HH * S == BANK and NT % (2 * CH) == 0

    x_tiles = x.rearrange("b s d -> (b s) d").rearrange("(t p) d -> p t d", p=P)
    ctx_rows = ctx.rearrange("b s d -> (b s) d")
    normed_tiles = normed.rearrange("(t p) d -> p t d", p=P)
    out_tiles = out[0:T, :].rearrange("(t p) d -> p t d", p=P)

    with ExitStack() as stack:
        def sb(name, shape, dtype=F32):
            return stack.enter_context(nc.sbuf_tensor(name, shape, dtype))

        def sem(name):
            return stack.enter_context(nc.semaphore(name))

        bank = [stack.enter_context(nc.psum_tensor(f"bank{i}", [P, BANK], F32)) for i in range(BANKS)]

        silu = sb("silu", [P, 2, CH * P])
        w_raw = silu[:, 0, :].rearrange("p (n d) -> p n d", n=4)
        w_t = sb("w_t", [P, 4, P])
        wr_sb = sb("wr_sb", [P, E])
        w1_sb = sb("w1_sb", [P, E + 1, F])
        w3_sb = sb("w3_sb", [P, E + 1, F])
        w2_sb = sb("w2_sb", [P, E + 1, FB, D])
        g_col = sb("g_col", [P, 1])
        b_col = sb("b_col", [P, 1])
        ident = sb("ident", [P, P])
        q_select = sb("q_select", [P, S], BF16)
        mask_u8 = sb("mask_u8", [P, S], U8)
        mask_bias = sb("mask_bias", [P, S], BF16)
        row_any = sb("row_any", [P, 1])
        group_mask = sb("group_mask", [P, G, P], F16)
        slot_mask = sb("slot_mask", [P, J, P], F16)
        j_index = silu[:, 1, :].rearrange("p (j n) -> p j n", j=J).bitcast(I32)
        p_index = sb("p_index", [P, 1], I32)
        p_head = sb("p_head", [P, 1], I32)
        p_head_f = sb("p_head_f", [P, 1])
        x_sb = sb("x_sb", [P, NT, D])
        ctx_sb = sb("ctx_sb", [P, 2, D])
        x1_now = sb("x1_now", [P, 2, D])
        stats_now = sb("stats_now", [P, 2, 6])
        stats_all = sb("stats_all", [P, NT, 6])
        sq_sum = sb("sq_sum", [P, NT])
        mean2 = sb("mean2", [P, NT])
        rstd = sb("rstd", [P, NT])
        shift = sb("shift", [P, NT])
        newton = sb("newton", [P, NT])
        variance = sb("variance", [P, NT])
        xn = sb("xn", [P, 2, D])
        xc_t = sb("xc_t", [P, 2, 2, P])
        qk_parts = sb("qk_parts", [P, 2, 2, P], F16)
        q_masked = sb("q_masked", [P, 2, 2, G, P], F16)
        k_masked = sb("k_masked", [P, 2, 2, J, P], F16)
        v_block = sb("v_block", [P, 2, 2, H // 2, 2, HD + 1])
        row_max = sb("row_max", [P, 2, HH])
        shifted = sb("shifted", [P, 2, HH, S])
        probs = sb("probs", [P, 2, 2, HH * S])
        probs_t = sb("probs_t", [P, 2, HH // 2, P])
        att_sum = sb("att_sum", [P, H])
        att_inv = sb("att_inv", [P, H])
        att = sb("att", [P, H, HD])
        att_t = sb("att_t", [P, P])
        t_sb = sb("t_sb", [P, 2, CH, D])
        h_t = sb("h_t", [P, NT * P])
        logits = sb("logits", [P, NT, E])
        CT = TOP_K * NT
        by_index = sb("by_index", [P, E])
        e_index = sb("e_index", [P, E])
        top = sb("top", [P, TOP_K, NT])
        eq = sb("eq", [P, NT, E])
        rest = sb("rest", [P, NT, E])
        pick = sb("pick", [P, NT])
        one_hot = sb("one_hot", [P, CT, E])
        one_hot_b = sb("one_hot_b", [P, CT, E], BF16)
        upto = sb("upto", [P, P], BF16)
        ones_b = sb("ones_b", [P, P], BF16)
        zeros = sb("zeros", [P, CT])
        totals = sb("totals", [P, CT, E])
        running = sb("running", [P, CT, E])
        place = sb("place", [P, CT, E])
        rank = sb("rank", [P, CT])
        expert = sb("expert", [P, CT])
        past1 = sb("past1", [P, CT])
        lo = sb("lo", [P, CT])
        keep = sb("keep", [P, CT])
        lo_b = sb("lo_b", [P, CT], BF16)
        blk_b = sb("blk_b", [P, CT], BF16)
        gates = sb("gates", [P, TOP_K, NT])
        gate_e = sb("gate_e", [P, NT])
        gate_d = sb("gate_d", [P, NT])
        LC = 8
        VALS = 5
        vals = sb("vals", [P, VALS, CT], BF16)
        gate_rest = sb("gate_rest", [P, CT])
        lane = sb("lane", [P, P, LC], BF16)
        blocks = sb("blocks", [P, NB, LC], BF16)
        at_lane = sb("at_lane", [P, 2, P, LC], BF16)
        at_block = sb("at_block", [P, NB, LC], BF16)
        carried = sb("carried", [P, 2, VALS, NB, LC], BF16)
        table = sb("table", [P, VALS, NB])
        used = sb("used", [P, NB])
        token = sb("token", [P, NB])
        spare = sb("spare", [P, NB])
        slot_gate = sb("slot_gate", [P, NB])
        from_row = sb("from_row", [P, NB], I32)
        to_row = sb("to_row", [P, NB], I32)
        p_index_f = sb("p_index_f", [P, 1])
        tile_index = sb("tile_index", [P, NT], I32)
        iota_i = sb("iota_i", [P, P], I32)
        zero_rows = sb("zero_rows", [P, D])
        XR = 3
        xe = sb("xe", [P, XR, EB, D])
        xe_t = sb("xe_t", [P, 2, EB, P])
        w_high = sb("w_high", [P, 2, 2, F], F32R)
        w_low = sb("w_low", [P, 2, 2, F], F32R)
        unit_parts = sb("unit_parts", [P, 2, 2, CH * P], F32R)
        gated = sb("gated", [P, 2, FB, CH * P])
        ye = sb("ye", [P, 2, EB, D])

        x_loaded = [sem("x_loaded0"), sem("x_loaded1")]
        w_loaded = sem("w_loaded")
        mask_loaded = sem("mask_loaded")
        small_loaded = sem("small_loaded")
        shared_loaded = sem("shared_loaded")
        experts_loaded = sem("experts_loaded")
        ctx_loaded = [sem("ctx_loaded0"), sem("ctx_loaded1")]
        pool_consts = sem("pool_consts")
        pool_step = sem("pool_step")
        dve_step = sem("dve_step")
        mask_ready = sem("mask_ready")
        w_transposed = sem("w_transposed")
        w_ready = sem("w_ready")
        xn_ready = sem("xn_ready")
        xc_transposed = sem("xc_transposed")
        xc_ready = sem("xc_ready")
        qk_projected = sem("qk_projected")
        qk_high = sem("qk_high")
        qk_low = sem("qk_low")
        qk_masked = sem("qk_masked")
        q_high_spread = sem("q_high_spread")
        x_scaled = sem("x_scaled")
        t_scaled = sem("t_scaled")
        v_projected = sem("v_projected")
        v_placed = sem("v_placed")
        scored = sem("scored")
        max_ready = sem("max_ready")
        shift_ready = sem("shift_ready")
        exp_ready = sem("exp_ready")
        p_transposed = sem("p_transposed")
        p_copied = sem("p_copied")
        att_summed = sem("att_summed")
        att_step = sem("att_step")
        att_ready = sem("att_ready")
        att_transposed = sem("att_transposed")
        att_copied = sem("att_copied")
        att_projected = sem("att_projected")
        x1_ready = sem("x1_ready")
        stats_ready = sem("stats_ready")
        x1_kept = sem("x1_kept")
        t_ready = sem("t_ready")
        t_stored = [sem("t_stored0"), sem("t_stored1")]
        t_transposed = sem("t_transposed")
        h_ready = sem("h_ready")
        routed = sem("routed")
        logits_ready = sem("logits_ready")
        gate_exp_in = sem("gate_exp_in")
        gate_exp = sem("gate_exp")
        onehot_ready = sem("onehot_ready")
        counted = sem("counted")
        carried_ready = sem("carried_ready")
        tabled = sem("tabled")
        table_ready = sem("table_ready")
        gathered = [sem(f"gathered{e}") for e in range(E)]
        w_high_ready = sem("w_high_ready")
        w_low_ready = sem("w_low_ready")
        w_low_shared = sem("w_low_shared")
        unit_high = sem("unit_high")
        unit_low = sem("unit_low")
        unit_low_shared = sem("unit_low_shared")
        up_done = sem("up_done")
        silu_ready = sem("silu_ready")
        gated_ready = sem("gated_ready")
        down_done = sem("down_done")
        summed = sem("summed")
        zero_ready = sem("zero_ready")
        out_stored = sem("out_stored")
        xe_transposed = sem("xe_transposed")
        xe_ready = sem("xe_ready")
        ye_ready = sem("ye_ready")
        scattered = sem("scattered")

        COUNT_SLOT = 10
        TABLE_SLOT = 18
        FIRST_GATHER_SLOT = 30
        CHUNKS_OF_SLOT = (2, 3), (4, 5), (6,), (7,)
        assert FB == len(CHUNKS_OF_SLOT) and NC == CHUNKS_OF_SLOT[-1][-1] + 1

        def down_bank(n, k):
            return bank[k][:, 0:P] if n == NC + E - 1 else bank[4 + n % 2][:, k * P:(k + 1) * P]

        def hidden_bank(c):
            return bank[(0, 3)[c] if c < 2 else 5 + c % 2]

        def w_float(m):
            e = m - 1 if m else E
            return w1_sb[:, e, :], w3_sb[:, e, :]

        def unit_float(n):
            if n < NC:
                return h_t[:, n * CH * P:(n + 1) * CH * P]
            return xe_t[:, (n - NC) % 2, :, :].rearrange("p k n -> p (k n)")

        def unit_part(n, part):
            return unit_parts[:, n % 2, part, 0:CH * P if n < NC else EB * P]

        block = stack.enter_context(nc.Block())

        FIRST, LAST = -3, NT + 3
        LOOP_FROM, LOOP_TO = 4, NT - 4
        SPLIT = 24

        def pipeline(engine, step, before=None):
            for i in range(FIRST, LOOP_FROM):
                if before and i in before:
                    before[i]()
                step(i, i % 2)
            if before and LOOP_FROM in before:
                before[LOOP_FROM]()
            with engine.Fori(LOOP_FROM // 2, LOOP_TO // 2, 1) as pair:
                step(pair * 2, 0)
                step(pair * 2 + 1, 1)
            for i in range(LOOP_TO, LAST):
                if before and i in before:
                    before[i]()
                step(i, i % 2)

        def live(n):
            return not isinstance(n, int) or 0 <= n < NT

        @block.sync
        def _(sp):
            q = NT // 4
            sp.dma_start(x_sb[:, 0:q, :], x_tiles[:, 0:q, :]).then_inc(x_loaded[0], 16)
            for n, w in enumerate((wq, wk, wv, wo)):
                sp.dma_start(w_raw[:, n, :], w).then_inc(w_loaded, 16)
            for n in range(2):
                sp.dma_start(mask_u8[n * S:(n + 1) * S, :], mask).then_inc(mask_loaded, 16)
            for n in range(2):
                sp.dma_start(ctx_sb[:, n, :], ctx_rows[n * P:(n + 1) * P, :]).then_inc(ctx_loaded[n], 16)
            for n in range(1, 4):
                sp.dma_start(x_sb[:, n * q:(n + 1) * q, :], x_tiles[:, n * q:(n + 1) * q, :]).then_inc(x_loaded[1], 16)
            sp.dma_start(g_col[:, :], ln_g.rearrange("(p a) -> p a", a=1)).then_inc(small_loaded, 16)
            sp.dma_start(b_col[:, :], ln_b.rearrange("(p a) -> p a", a=1)).then_inc(small_loaded, 16)
            sp.dma_start(wr_sb[:, :], wr).then_inc(small_loaded, 16)
            sp.dma_start(w1_sb[:, E, :], w1s).then_inc(shared_loaded, 16)
            sp.dma_start(w3_sb[:, E, :], w3s).then_inc(shared_loaded, 16)
            sp.dma_start(w2_sb[:, E, :, :], w2s.rearrange("(f p) d -> p f d", p=P)).then_inc(shared_loaded, 16)

            with sp.Fori(1, NT // 2, 1) as pair:
                for par in range(2):
                    n = pair * 2 + par
                    sp.wait_ge(xc_transposed, n - 1)
                    sp.dma_start(ctx_sb[:, par, :], ctx_rows[bass.ds(n * P, P), :]).then_inc(ctx_loaded[par], 16)
            sp.dma_start(w1_sb[:, 0:E, :], w1.rearrange("e d f -> d e f")).then_inc(experts_loaded, 16)
            sp.dma_start(w3_sb[:, 0:E, :], w3.rearrange("e d f -> d e f")).then_inc(experts_loaded, 16)
            sp.dma_start(w2_sb[:, 0:E, :, :].rearrange("p e f d -> p (e f) d"), w2.rearrange("e (f p) d -> p (e f) d", p=P)).then_inc(experts_loaded, 16)
            with sp.Fori(0, NC // 2, 1) as pair:
                n = pair * 2
                for par in range(2):
                    sp.wait_ge(t_ready, n + (par + 1))
                    sp.dma_start(normed_tiles[:, bass.ds((n + par) * CH, CH), :], t_sb[:, par, :, :])\
                      .then_inc(t_stored[par], 16)
            sp.wait_ge(zero_ready, 1)
            sp.dma_start(out[T:T + P, :], zero_rows[:, :]).then_inc(out_stored, 16)
            with sp.Fori(0, NC, 1) as c:
                sp.wait_ge(summed, c + 1)
                sp.dma_start(out_tiles[:, bass.ds(c * CH, CH), :], x_sb[:, bass.ds(c * CH, CH), :]).then_inc(out_stored, 16)
            sp.wait_ge(scattered, 16 * EB * E)

        @block.gpsimd
        def _(pool):
            def const(ins):
                ins.then_inc(pool_step, 1)

            const(pool.memset(ident[:, :], 0.0))
            pool.wait_ge(pool_step, 1)
            pool.affine_select(out=ident[:, :], in_=ident[:, :], compare_op=ALU.not_equal, fill=1.0, base=0,
                               pattern=[[-1, P]], channel_multiplier=1).then_inc(pool_consts, 1)
            const(pool.memset(v_block[:], 0.0))
            const(pool.memset(group_mask[:], 0.0))
            const(pool.memset(q_masked[:], 0.0))
            const(pool.memset(upto[:, :], 1.0))
            const(pool.memset(mask_bias[:, :], 0.0))
            pool.wait_ge(pool_step, 6)
            done = [1]

            def apart(ins):
                done[0] += 1
                ins.then_inc(pool_consts, 1)
                pool.wait_ge(pool_consts, done[0])

            for half in range(2):
                for par in range(2):
                    for b in range(2):
                        apart(pool.memset(v_block[half * S:(half + 1) * S, par, b, :, half, HD:HD + 1], 1.0))
            for g in range(G):
                apart(pool.memset(group_mask[g * 32:(g + 1) * 32, g, :], 1.0))
            pool.affine_select(out=upto[:, :], in_=upto[:, :], compare_op=ALU.is_ge, fill=0.0, base=0,
                               pattern=[[1, P]], channel_multiplier=-1).then_inc(pool_consts, 1)
            pool.iota(j_index, pattern=[[1, J], [0, P]], base=0, channel_multiplier=0).then_inc(pool_consts, 1)
            pool.iota(p_index[:, :], pattern=[[0, 1]], base=0, channel_multiplier=1).then_inc(pool_consts, 1)
            pool.iota(iota_i[:, :], pattern=[[1, P]], base=0, channel_multiplier=0).then_inc(pool_consts, 1)
            pool.iota(tile_index[:, :], pattern=[[1, NT]], base=1, channel_multiplier=0).then_inc(pool_consts, 1)
            pool.memset(ones_b[:, :], 1.0).then_inc(pool_consts, 1)
            pool.memset(zeros[:, :], 0.0).then_inc(pool_consts, 1)
            pool.memset(zero_rows[:, :], 0.0).then_inc(zero_ready, 1)

            def keep_tile(n, par):
                at_least(pool, stats_ready, n + 1)
                pool.tensor_copy(x_sb[:, bass.ds(n, 1), :].rearrange("p a d -> p (a d)"), x1_now[:, par, :])
                pool.tensor_copy(stats_all[:, bass.ds(n, 1), :].rearrange("p a d -> p (a d)"), stats_now[:, par, :])\
                    .then_inc(x1_kept, 1)

            with pool.Fori(0, NT // 2 - 1, 1) as pair:
                keep_tile(pair * 2, 0)
                keep_tile(pair * 2 + 1, 1)
            pool.wait_ge(w_high_ready, 1)
            for k in range(2):
                pool.tensor_tensor(w_low[:, 0, k, :], w_float(0)[k], w_high[:, 0, k, :].bitcast(F32), ALU.subtract)\
                    .then_inc(w_low_shared, 1)
                keep_tile(NT - 2 + k, k)
            for n in range(1, NC):
                pool.wait_ge(unit_high, n + 1)
                pool.tensor_tensor(unit_part(n, 1), unit_float(n), unit_part(n, 0).bitcast(F32), ALU.subtract)\
                    .then_inc(unit_low_shared, 1)

            pool.wait_ge(table_ready, 1)
            for par in range(2):
                pool.wait_ge(t_stored[par], 16 * (NC // 2))

            def gather(e):
                at_least(pool, xe_transposed, e - XR + 1)
                for k in range(EB):
                    s = e * EB + k
                    pool.indirect_dma_start(xe[:, e % XR, k, :], None, normed,
                                            bass.IndirectOffsetOnAxis(ap=from_row[:, s:s + 1].bitcast(U32), axis=0))\
                        .then_inc(gathered[e], 16)

            for e in range(XR):
                gather(e)
            pool.wait_ge(out_stored, 16 * (NC + 1))
            for e in range(E):
                if e + XR < E:
                    gather(e + XR)
                at_least(pool, scattered, 16 * EB * e)
                for k in range(EB):
                    s = e * EB + k
                    pool.wait_ge(ye_ready, s + 1)
                    pool.indirect_dma_start(out, bass.IndirectOffsetOnAxis(ap=to_row[:, s:s + 1].bitcast(U32), axis=0),
                                            ye[:, e % 2, k, :], None, compute_op=ALU.add).then_inc(scattered, 16)

        POOL_CONSTS = 1 + 8 + G + 1 + 4 + 2

        @block.tensor
        def _(pe):
            pe.wait_ge(pool_consts, 1)
            pe.wait_ge(w_loaded, 64)
            for n in range(4):
                ins = pe.transpose(bank[0][:, n * P:(n + 1) * P], w_raw[:, n, :], ident[:, :])
            ins.then_inc(w_transposed, 1)
            pe.wait_ge(w_ready, 1)

            def transpose_inputs(n, par):
                at_least(pe, qk_low, n)
                pe.wait_ge(ctx_loaded[par], (n // 2 + 1) * 16 if isinstance(n, int) else (n - par) * 8 + 16)
                at_least(pe, xn_ready, n + 1)
                pe.transpose(bank[2][:, 0:P], xn[:, par, :], ident[:, :])
                pe.transpose(bank[2][:, P:2 * P], ctx_sb[:, par, :], ident[:, :]).then_inc(xc_transposed, 1)

            def project_qk(n, par):
                at_least(pe, xc_ready, n + 1)
                pe.matmul(bank[2][:, 2 * P:3 * P], w_t[:, 0, :], xc_t[:, par, 0, :], start=True, stop=True)
                pe.matmul(bank[2][:, 3 * P:4 * P], w_t[:, 1, :], xc_t[:, par, 1, :], start=True, stop=True)\
                  .then_inc(qk_projected, 1)

            def project_v(n, par):
                at_least(pe, v_placed, n * 2)
                for b in range(2):
                    for half in range(2):
                        ins = pe.matmul(bank[3][half * S:(half + 1) * S, b * P:(b + 1) * P],
                                        xc_t[:, par, 1, b * S:(b + 1) * S], w_t[:, 2, :], start=True, stop=True)
                ins.then_inc(v_projected, 1)

            def score(n, par, half):
                if isinstance(n, int) and n == 0 and half == 0:
                    pe.wait_ge(mask_ready, 1)
                if half == 0:
                    at_least(pe, qk_masked, n + 1)
                    at_least(pe, q_high_spread, n + 1)
                at_least(pe, shift_ready, n * 2 + (half - 1))
                for b in range(2):
                    pe.matmul(bank[half][b * S:(b + 1) * S, :], q_select[:, :],
                              mask_bias[:, :].unsqueeze(1).to_broadcast([P, HH, S]), start=True, stop=False)
                for gl in range(2):
                    for m, (qp, kp) in enumerate(((0, 0), (0, 1), (1, 0))):
                        for b in range(2):
                            ins = pe.matmul(bank[half][b * S:(b + 1) * S, gl * J * S:(gl + 1) * J * S],
                                            q_masked[:, par, qp, half * 2 + gl, b * S:(b + 1) * S],
                                            k_masked[:, par, kp, :, b * S:(b + 1) * S],
                                            start=False, stop=(gl == 1 and m == 2))
                ins.then_inc(scored, 1)

            def transpose_probs(n, par, half):
                at_least(pe, exp_ready, n * 2 + (half + 1))
                at_least(pe, p_copied, n * 2 + (half - 1))
                for c in range(HH // 2):
                    ins = pe.transpose(bank[4 + half][:, c * P:(c + 1) * P],
                                       probs[:, par, half, c * P:(c + 1) * P], ident[:, :])
                ins.then_inc(p_transposed, 1)

            def weigh_values(n, par, half):
                at_least(pe, p_copied, n * 2 + (half + 1))
                if half == 0:
                    at_least(pe, v_placed, n * 2 + 2)
                    at_least(pe, att_ready, n)
                W = 2 * (HD + 1)
                for c in range(HH // 2):
                    pair = half * (HH // 2) + c
                    for b in range(2):
                        ins = pe.matmul(bank[6][b * S:(b + 1) * S, pair * W:(pair + 1) * W],
                                        probs_t[:, half, c, b * S:(b + 1) * S],
                                        v_block[:, par, b, pair, :, :].rearrange("p a d -> p (a d)"),
                                        start=True, stop=True)
                ins.then_inc(att_summed, 1)

            def transpose_att(n):
                at_least(pe, att_ready, n + 1)
                at_least(pe, x1_ready, n)
                pe.transpose(bank[7][:, 0:P], att[:, :, :].rearrange("p h d -> p (h d)"), ident[:, :])\
                  .then_inc(att_transposed, 1)

            def project_out(n):
                at_least(pe, att_copied, n + 1)
                pe.matmul(bank[7][:, P:2 * P], att_t[:, :], w_t[:, 3, :], start=True, stop=True)\
                  .then_inc(att_projected, 1)

            def step(i, par):
                if live(i + 1):
                    project_qk(i + 1, 1 - par)
                if live(i):
                    score(i, par, 0)
                if live(i + 2):
                    transpose_inputs(i + 2, par)
                if live(i - 1):
                    transpose_probs(i - 1, 1 - par, 0)
                if live(i - 2):
                    transpose_att(i - 2)
                if live(i - 1):
                    transpose_probs(i - 1, 1 - par, 1)
                if live(i):
                    score(i, par, 1)
                if live(i - 1):
                    weigh_values(i - 1, 1 - par, 0)
                if live(i - 2):
                    project_out(i - 2)
                if live(i - 1):
                    weigh_values(i - 1, 1 - par, 1)
                if live(i + 1):
                    project_v(i + 1, 1 - par)

            def to_hidden(c):
                pe.wait_ge(t_ready, c + 1)
                if c == 0:
                    pe.wait_ge(shift_ready, NT * 2 - 1)
                elif c == 1:
                    pe.wait_ge(v_placed, NT * 2)
                elif c == 3:
                    pe.wait_ge(att_ready, NT)
                else:
                    pe.wait_ge(h_ready, c - 1)
                for k in range(CH):
                    ins = pe.transpose(hidden_bank(c)[:, k * P:(k + 1) * P], t_sb[:, c % 2, k, :], ident[:, :])
                ins.then_inc(t_transposed, 1)

            def route(c):
                pe.wait_ge(h_ready, c + 1)
                if c == 0:
                    pe.wait_ge(x1_ready, NT)
                at_least(pe, logits_ready, c)
                for k in range(CH):
                    t = c * CH + k
                    ins = pe.matmul(bank[7][:, k * E:(k + 1) * E], h_t[:, t * P:(t + 1) * P], wr_sb[:, :],
                                    start=True, stop=True)
                ins.then_inc(routed, 1)

            def count_choices():
                pe.wait_ge(onehot_ready, 1)
                flat = one_hot_b[:, :, :].rearrange("p c e -> p (c e)")
                pe.matmul(bank[6][:, 0:CT * E], upto[:, :], flat, start=True, stop=True)
                pe.matmul(bank[7][:, 0:CT * E], ones_b[:, :], flat, start=True, stop=True).then_inc(counted, 1)

            def fill_table(part):
                pe.wait_ge(carried_ready, part + 1)
                for ct in range(part * LC, (part + 1) * LC):
                    half = ct // LC % 2
                    ins = pe.matmul(bank[6][:, 0:VALS * NB], at_lane[:, half, :, ct % LC],
                                    carried[:, half, :, :, ct % LC].rearrange("p v n -> p (v n)"),
                                    start=(ct == 0), stop=(ct == CT - 1))
                ins.then_inc(tabled, 1)

            def up(n, f):
                m = max(n - NC + 1, 0)
                if f == 0:
                    pe.wait_ge(unit_high, n + 1)
                    if n == 0:
                        pe.wait_ge(w_low_shared, 2)
                        pe.wait_ge(unit_low, 1)
                    elif n < NC:
                        pe.wait_ge(unit_low_shared, n)
                    else:
                        pe.wait_ge(w_low_ready, m)
                        pe.wait_ge(unit_low, m + 1)
                at_least(pe, gated_ready, n * FB + (f - 1))
                high, low = unit_part(n, 0), unit_part(n, 1)
                width, columns = high.shape[1], slice(f * P, (f + 1) * P)
                for k in range(2):
                    into = bank[2 * (f % 2) + k][:, 0:width]
                    pe.matmul(into, w_high[:, m % 2, k, columns], high, start=True, stop=False)
                    pe.matmul(into, w_high[:, m % 2, k, columns], low, start=False, stop=False)
                    ins = pe.matmul(into, w_low[:, m % 2, k, columns], high, start=False, stop=True)
                ins.then_inc(up_done, 1)

            def down(n, k, e, tiles):
                if k >= tiles:
                    return
                if k == 0:
                    pe.wait_ge(gated_ready, n * FB + FB)
                    at_least(pe, summed, min(n - 1, NC))
                    at_least(pe, ye_ready, (n - 1 - NC) * EB)
                for f in range(FB):
                    ins = pe.matmul(down_bank(n, k), gated[:, n % 2, f, k * P:(k + 1) * P],
                                    w2_sb[:, e, f, :], start=(f == 0), stop=(f == FB - 1))
                ins.then_inc(down_done, 1)

            def transpose_slots(e):
                pe.wait_ge(gathered[e], 16 * EB)
                at_least(pe, xe_ready, e)
                for k in range(EB):
                    ins = pe.transpose(bank[7][:, k * P:(k + 1) * P], xe[:, e % XR, k, :], ident[:, :])
                ins.then_inc(xe_transposed, 1)

            def shared_slot(n, f):
                up(n, f)
                if n:
                    down(n - 1, f, E, CH)

            def first_slot():
                pe.wait_ge(shared_loaded, 48)
                shared_slot(0, 0)

            pipeline(pe, step, {NT: lambda: to_hidden(0), NT + 1: lambda: to_hidden(1), NT + 2: first_slot})
            for f in range(FB):
                if f:
                    shared_slot(0, f)
                for c in CHUNKS_OF_SLOT[f]:
                    route(c - 2)
                    to_hidden(c)
            route(NC - 2)
            for n in range(1, NC):
                for f in range(FB):
                    slot = n * FB + f
                    shared_slot(n, f)
                    if slot == FB:
                        route(NC - 1)
                    if slot == COUNT_SLOT:
                        count_choices()
                    if TABLE_SLOT <= slot < TABLE_SLOT + CT // LC:
                        fill_table(slot - TABLE_SLOT)
                    if slot == FIRST_GATHER_SLOT:
                        transpose_slots(0)

            pe.wait_ge(experts_loaded, 48)
            for e in range(E):
                for f in range(FB):
                    up(NC + e, f)
                    down(NC + e - 1, f, e - 1 if e else E, EB if e else CH)
                    if f == 1 and e + 1 < E:
                        transpose_slots(e + 1)
            for k in range(EB):
                down(NC + E - 1, k, E - 1, EB)

        @block.scalar
        def _(act):
            act.wait_ge(w_transposed, 1)
            act.activation(w_t[:, :, :], bank[0][:, :].rearrange("p (n m) -> p n m", n=4), ACT.Copy).then_inc(w_ready, 1)

            def normalise(n, par):
                if isinstance(n, int) and n == 0:
                    act.wait_ge(x_scaled, 1)
                at_least(act, xc_transposed, n - 1)
                act.activation(xn[:, par, :], x_sb[:, bass.ds(n, 1), :].rearrange("p a d -> p (a d)"), ACT.Identity,
                               scale=rstd[:, bass.ds(n, 1)], bias=shift[:, bass.ds(n, 1)]).then_inc(xn_ready, 1)

            def copy_inputs(n, par):
                at_least(act, xc_transposed, n + 1)
                act.activation(xc_t[:, par, :, :], bank[2][:, 0:2 * P].rearrange("p (a n) -> p a n", a=2), ACT.Copy)\
                   .then_inc(xc_ready, 1)

            def copy_att(n):
                at_least(act, att_transposed, n + 1)
                act.activation(att_t[:, :], bank[7][:, 0:P], ACT.Copy).then_inc(att_copied, 1)

            def copy_probs(n, half):
                at_least(act, p_transposed, n * 2 + (half + 1))
                at_least(act, att_summed, n * 2 + (half - 1))
                act.activation(probs_t[:, half, :, :], bank[4 + half][:, :].rearrange("p (c n) -> p c n", n=P), ACT.Copy)\
                   .then_inc(p_copied, 1)

            def high_parts(n):
                at_least(act, qk_projected, n + 1)
                at_least(act, qk_masked, n)
                act.activation(qk_parts[:, 0, :, :], bank[2][:, 2 * P:4 * P].rearrange("p (a n) -> p a n", a=2), ACT.Copy)\
                   .then_inc(qk_high, 1)

            def spread_q_high(n, par):
                at_least(act, scored, n * 2 - 2)
                at_least(act, qk_high, n + 1)
                for g in range(G):
                    rows = slice(g * 32, (g + 1) * 32)
                    ins = act.activation(q_masked[rows, par, 0, g, :], qk_parts[rows, 0, 0, :], ACT.Copy)
                ins.then_inc(q_high_spread, 1)

            def exponentials(n, par, half):
                at_least(act, shift_ready, n * 2 + (half + 1))
                act.activation(probs[:, par, half, :], shifted[:, half, :, :].rearrange("p h k -> p (h k)"), ACT.Exp,
                               scale=SCALE).then_inc(exp_ready, 1)

            def place_values(n, par):
                at_least(act, v_projected, n + 1)
                for half in range(2):
                    rows = slice(half * S, (half + 1) * S)
                    ins = act.activation(
                        v_block[rows, par, :, :, half, 0:HD].rearrange("p b h d -> p (b h) d"),
                        bank[3][rows, 0:2 * P].rearrange("p (h a d) -> p h a d", a=2, d=HD)[:, :, half, :], ACT.Copy)
                    ins.then_inc(v_placed, 1)

            def step(i, par):
                if live(i + 1):
                    high_parts(i + 1)
                if live(i - 1):
                    exponentials(i - 1, 1 - par, 1)
                if live(i + 1):
                    spread_q_high(i + 1, 1 - par)
                if live(i + 2):
                    copy_inputs(i + 2, par)
                if live(i - 1):
                    copy_probs(i - 1, 0)
                if live(i - 2):
                    copy_att(i - 2)
                if live(i):
                    place_values(i, par)
                if live(i - 1):
                    copy_probs(i - 1, 1)
                if live(i + 3):
                    normalise(i + 3, 1 - par)
                if live(i):
                    exponentials(i, par, 0)

            def normalise_chunk(c):
                if c * CH in (0, SPLIT):
                    act.wait_ge(t_scaled, 1 + (c * CH) // SPLIT)
                at_least(act, t_transposed, c - 1)
                at_least(act, t_stored[c % 2], c // 2 * 16)
                for t in range(c * CH, (c + 1) * CH):
                    ins = act.activation(t_sb[:, c % 2, t % CH, :], x_sb[:, t, :], ACT.Identity,
                                         scale=rstd[:, t:t + 1], bias=shift[:, t:t + 1])
                ins.then_inc(t_ready, 1)

            def split_weights(m):
                if m == 0:
                    act.wait_ge(shared_loaded, 48)
                elif m == 1:
                    act.wait_ge(experts_loaded, 48)
                else:
                    act.wait_ge(up_done, (NC + m - 2) * FB)
                for k in range(2):
                    ins = act.activation(w_high[:, m % 2, k, :], w_float(m)[k], ACT.Copy)
                ins.then_inc(w_high_ready, 1)

            def split_unit(n):
                if n < NC:
                    act.wait_ge(h_ready, n + 1)
                else:
                    act.wait_ge(xe_ready, n - NC + 1)
                at_least(act, up_done, (n - 1) * FB)
                act.activation(unit_part(n, 0), unit_float(n), ACT.Copy).then_inc(unit_high, 1)

            act.wait_ge(pool_consts, POOL_CONSTS)
            pipeline(act, step, {LOOP_FROM: lambda: act.wait_ge(x_scaled, 2),
                                 NT - 3: lambda: split_weights(0),
                                 NT - 1: lambda: normalise_chunk(0), NT: lambda: normalise_chunk(1),
                                 NT + 1: lambda: split_unit(0)})

            def silu_slot(n, f, width):
                act.wait_ge(up_done, n * FB + (f + 1))
                at_least(act, gated_ready, n * FB + (f - 1))
                act.activation(silu[:, f % 2, 0:width], bank[2 * (f % 2)][:, 0:width], ACT.Silu)\
                   .then_inc(silu_ready, 1)

            normalise_chunk(2)
            for f in range(FB):
                silu_slot(0, f, CH * P)
                for c in (CHUNKS_OF_SLOT[0][1:] + CHUNKS_OF_SLOT[1][:1], CHUNKS_OF_SLOT[1][1:], *CHUNKS_OF_SLOT[2:])[f]:
                    normalise_chunk(c)
                if f == 1:
                    split_unit(1)
            for n in range(1, NC + E):
                when = 1 if n + 1 < NC else 3 if n + 1 == NC else 2
                for f in range(FB):
                    silu_slot(n, f, (CH if n < NC else EB) * P)
                    if f == when and n + 1 < NC + E:
                        split_unit(n + 1)
                    if f == 0 and NC <= n + 1 < NC + E:
                        split_weights(n + 2 - NC)
                if n == 2:
                    act.wait_ge(gate_exp_in, 1)
                    act.activation(gate_e[:, :], gate_d[:, :], ACT.Exp).then_inc(gate_exp, 1)

        @block.vector
        def _(dve):
            chain = Chain(dve, dve_step)
            then = chain.then

            def newton_steps(out_, v, scratch, steps):
                for _ in range(steps):
                    then(dve.tensor_tensor(scratch, out_, out_, ALU.mult))
                    then(dve.scalar_tensor_tensor(out=scratch, in0=scratch, scalar=-0.5, in1=v, op0=ALU.mult, op1=ALU.mult))
                    then(dve.scalar_tensor_tensor(out=out_, in0=scratch, scalar=1.5, in1=out_, op0=ALU.add, op1=ALU.mult))

            def start_scales(tiles, factor, constant):
                even, odd = stats_all[:, tiles, 1], stats_all[:, tiles, 4]
                scratch, root = newton[:, tiles], rstd[:, tiles].bitcast(I32)
                dve.tensor_tensor(sq_sum[:, tiles], stats_all[:, tiles, 2], stats_all[:, tiles, 5], ALU.add)
                dve.tensor_tensor(mean2[:, tiles], even, odd, ALU.add)
                then(dve.tensor_tensor(scratch, even, odd, ALU.subtract))
                then(dve.tensor_tensor(scratch, scratch, scratch, ALU.mult))
                then(dve.scalar_tensor_tensor(out=sq_sum[:, tiles], in0=scratch, scalar=D / 4.0, in1=sq_sum[:, tiles],
                                              op0=ALU.mult, op1=ALU.add))
                then(dve.tensor_scalar(variance[:, tiles], sq_sum[:, tiles], factor / D, constant, ALU.mult, ALU.add))
                then(dve.tensor_scalar(root, variance[:, tiles].bitcast(I32), 1, None, ALU.logical_shift_right))
                then(dve.tensor_scalar(root, root, -1.0, float(0x5f3759df), ALU.mult, ALU.add))

            def finish_scales(tiles):
                newton_steps(rstd[:, tiles], variance[:, tiles], newton[:, tiles], 3)
                return dve.scalar_tensor_tensor(out=shift[:, tiles], in0=mean2[:, tiles], scalar=-0.5,
                                                in1=rstd[:, tiles], op0=ALU.mult, op1=ALU.mult)

            def input_stats(first, last):
                for n in range(first, last):
                    ins = dve.bn_stats(stats_all[:, n, :], x_sb[:, n, :])
                then(ins)

            Q = NT // 4
            dve.wait_ge(x_loaded[0], 16)
            input_stats(0, Q)
            start_scales(slice(0, Q), 1.0, EPS)
            finish_scales(slice(0, Q)).then_inc(x_scaled, 1)

            dve.wait_ge(pool_step, 6)
            dve.wait_ge(mask_loaded, 16 * 2)
            then(dve.tensor_scalar(mask_bias[0:S, :], mask_u8[0:S, :], -1.0, 1e9 / SCALE, ALU.add, ALU.mult))
            then(dve.tensor_reduce(row_any[:, :], mask_u8[:, :], X, ALU.max))
            dve.wait_ge(pool_consts, POOL_CONSTS)
            then(dve.tensor_copy(q_select[:, :], ident[:, 0:S]))
            then(dve.tensor_scalar(p_head[:, :], p_index[:, :], 3, J - 1, ALU.logical_shift_right, ALU.bitwise_and))
            then(dve.tensor_copy(p_head_f[:, :], p_head[:, :]))
            dve.tensor_scalar(slot_mask[:, :, :], j_index[:, :, :], p_head_f[:, 0:1], None, ALU.is_equal)\
               .then_inc(mask_ready, 1)
            dve.wait_ge(mask_ready, 1)

            def find_max(n, half):
                at_least(dve, scored, n * 2 + (half + 1))
                at_least(dve, shift_ready, n * 2 + (half - 1))
                dve.tensor_reduce(row_max[:, half, :], bank[half][:, :].rearrange("p (h k) -> p h k", k=S), X, ALU.max)\
                   .then_inc(max_ready, 1)

            def subtract_max(n, half):
                at_least(dve, max_ready, n * 2 + (half + 1))
                at_least(dve, exp_ready, n * 2 + (half - 1))
                dve.tensor_tensor(shifted[:, half, :, :], bank[half][:, :].rearrange("p (h k) -> p h k", k=S),
                                  row_max[:, half, :].unsqueeze(2).to_broadcast([P, HH, S]), ALU.subtract)\
                   .then_inc(shift_ready, 1)

            def low_parts(n):
                at_least(dve, qk_high, n + 1)
                at_least(dve, qk_masked, n)
                dve.tensor_tensor(qk_parts[:, 1, :, :], bank[2][:, 2 * P:4 * P].rearrange("p (a n) -> p a n", a=2),
                                  qk_parts[:, 0, :, :], ALU.subtract).then_inc(qk_low, 1)

            def spread_q_low(n, par):
                at_least(dve, scored, n * 2 - 2)
                at_least(dve, qk_low, n + 1)
                dve.tensor_tensor(q_masked[:, par, 1, :, :], qk_parts[:, 1, 0, :].unsqueeze(1).to_broadcast([P, G, P]),
                                  group_mask[:, :, :], ALU.mult)

            def spread_k(n, par):
                dve.tensor_tensor(k_masked[:, par, :, :, :],
                                  qk_parts[:, :, 1, :].unsqueeze(2).to_broadcast([P, 2, J, P]),
                                  slot_mask[:, :, :].unsqueeze(1).to_broadcast([P, 2, J, P]), ALU.mult)\
                   .then_inc(qk_masked, 1)

            sums = bank[6][:, 0:H * (HD + 1)].rearrange("p (h d) -> p h d", d=HD + 1)

            def read_sums(n):
                at_least(dve, att_summed, n * 2 + 2)
                at_least(dve, att_ready, n)
                dve.tensor_scalar(att_sum[:, :], sums[:, :, HD], 1e-9, None, ALU.max).then_inc(att_step, 1)

            def invert_sums(n):
                dve.wait_ge(att_step, n * 2 + 1)
                dve.reciprocal(att_inv[:, :], att_sum[:, :]).then_inc(att_step, 1)

            def divide_by_sums(n):
                dve.wait_ge(att_step, n * 2 + 2)
                dve.scalar_tensor_tensor(out=att[:, :, :], in0=sums[:, :, 0:HD], scalar=row_any[:, 0:1],
                                         in1=att_inv[:, :].unsqueeze(2).to_broadcast([P, H, HD]),
                                         op0=ALU.mult, op1=ALU.mult).then_inc(att_ready, 1)

            def add_residual(n, par):
                at_least(dve, att_projected, n + 1)
                at_least(dve, x1_kept, n - 1)
                dve.tensor_tensor(x1_now[:, par, :], x_sb[:, bass.ds(n, 1), :].rearrange("p a d -> p (a d)"),
                                  bank[7][:, P:2 * P], ALU.add).then_inc(x1_ready, 1)

            def take_stats(n, par):
                at_least(dve, x1_ready, n + 1)
                dve.bn_stats(stats_now[:, par, :], x1_now[:, par, :]).then_inc(stats_ready, 1)

            def step(i, par):
                if live(i - 3):
                    add_residual(i - 3, 1 - par)
                if live(i - 2):
                    read_sums(i - 2)
                if live(i + 1):
                    low_parts(i + 1)
                if live(i - 2):
                    invert_sums(i - 2)
                if live(i + 1):
                    spread_q_low(i + 1, 1 - par)
                if live(i - 2):
                    divide_by_sums(i - 2)
                if live(i + 1):
                    spread_k(i + 1, 1 - par)
                if live(i):
                    find_max(i, 0)
                if live(i - 3):
                    take_stats(i - 3, 1 - par)
                if live(i):
                    subtract_max(i, 0)
                    find_max(i, 1)
                    subtract_max(i, 1)

            def start_token_scales(first, last):
                dve.wait_ge(x1_kept, last)
                start_scales(slice(first, last), 1.0 + EPS, EPS * EPS)

            def finish_token_scales(first, last):
                finish_scales(slice(first, last)).then_inc(t_scaled, 1)

            def scale_chunk(c):
                dve.wait_ge(t_transposed, c + 1)
                dve.tensor_scalar(h_t[:, c * CH * P:(c + 1) * CH * P], hidden_bank(c)[:, :], g_col[:, 0:1],
                                  b_col[:, 0:1], ALU.mult, ALU.add).then_inc(h_ready, 1)

            def lower_unit(n):
                dve.wait_ge(unit_high, n + 1)
                dve.tensor_tensor(unit_part(n, 1), unit_float(n), unit_part(n, 0).bitcast(F32), ALU.subtract)\
                   .then_inc(unit_low, 1)

            def other_stats(n):
                if n == 1:
                    dve.wait_ge(x_loaded[1], 16 * 3)
                input_stats(n * Q, (n + 1) * Q)

            others = slice(Q, NT)

            def first_chunk():
                dve.wait_ge(small_loaded, 16 * 3)
                scale_chunk(0)

            def second_chunk():
                lower_unit(0)
                scale_chunk(1)

            pipeline(dve, step, {-1: lambda: other_stats(1), 0: lambda: other_stats(2), 1: lambda: other_stats(3),
                                 2: lambda: start_scales(others, 1.0, EPS),
                                 3: lambda: finish_scales(others).then_inc(x_scaled, 1),
                                 NT - 3: lambda: start_token_scales(0, SPLIT),
                                 NT - 2: lambda: finish_token_scales(0, SPLIT),
                                 NT + 1: first_chunk, NT + 2: second_chunk})
            def keep_logits(c):
                dve.wait_ge(routed, c + 1)
                dve.tensor_copy(logits[:, c * CH:(c + 1) * CH, :],
                                bank[7][:, 0:CH * E].rearrange("p (k e) -> p k e", k=CH)).then_inc(logits_ready, 1)

            spread = [P, NT, E]

            def largest(c):
                source = logits
                if c:
                    then(dve.scalar_tensor_tensor(out=rest[:, :, :], in0=one_hot[:, 0:NT, :], scalar=-3e38,
                                                  in1=logits[:, :, :], op0=ALU.mult, op1=ALU.add))
                    source = rest
                then(dve.tensor_reduce(top[:, c, :], source[:, :, :], X, ALU.max))
                then(dve.tensor_tensor(eq[:, :, :], source[:, :, :], top[:, c, :].unsqueeze(2).to_broadcast(spread),
                                       ALU.is_equal))

            def choose(c):
                then(dve.tensor_tensor(eq[:, :, :], eq[:, :, :], by_index[:, :].unsqueeze(1).to_broadcast(spread), ALU.mult))
                then(dve.tensor_reduce(pick[:, :], eq[:, :, :], X, ALU.max))
                then(dve.tensor_tensor(one_hot[:, c * NT:(c + 1) * NT, :], eq[:, :, :],
                                       pick[:, :].unsqueeze(2).to_broadcast(spread), ALU.is_equal))

            def pass_choices():
                dve.tensor_copy(one_hot_b[:, :, :], one_hot[:, :, :]).then_inc(onehot_ready, 1)
                dve.tensor_tensor(gate_d[:, :], top[:, 1, :], top[:, 0, :], ALU.subtract).then_inc(gate_exp_in, 1)

            def index_tables():
                then(dve.tensor_copy(e_index[:, :], iota_i[:, 0:E]))
                then(dve.tensor_scalar(by_index[:, :], e_index[:, :], -1.0, float(E), ALU.mult, ALU.add))
                for c in range(TOP_K):
                    then(dve.tensor_copy(vals[:, 0, c * NT:(c + 1) * NT], tile_index[:, :]))
                then(dve.tensor_copy(p_index_f[:, :], p_index[:, :]))
                then(dve.tensor_copy(vals[:, 1, :], p_index_f[:, 0:1].to_broadcast([P, CT])))
                dve.tensor_copy(lane[:, :, :], iota_i[:, :].unsqueeze(2).to_broadcast([P, P, LC]))
                then(dve.tensor_copy(blocks[:, :, :], iota_i[:, 0:NB].unsqueeze(2).to_broadcast([P, NB, LC])))

            def sum_tiles(experts):
                if 0 in experts:
                    dve.wait_ge(counted, 1)
                    then(dve.tensor_copy(totals[:, :, :], bank[7][:, 0:CT * E].rearrange("p (c e) -> p c e", e=E)))
                for e in experts:
                    ins = dve.tensor_tensor_scan(running[:, :, e], totals[:, :, e], zeros[:, :], 0.0, ALU.add, ALU.add)
                then(ins)

            def place_choices():
                then(dve.tensor_tensor(running[:, :, :], running[:, :, :], totals[:, :, :], ALU.subtract))
                then(dve.tensor_tensor(place[:, :, :], bank[6][:, 0:CT * E].rearrange("p (c e) -> p c e", e=E),
                                       running[:, :, :], ALU.add))

            def rank_choices():
                then(dve.tensor_tensor(place[:, :, :], place[:, :, :], one_hot[:, :, :], ALU.mult))
                then(dve.tensor_reduce(rank[:, :], place[:, :, :], X, ALU.add))

            def name_experts():
                then(dve.tensor_tensor(running[:, :, :], one_hot[:, :, :],
                                       e_index[:, :].unsqueeze(1).to_broadcast([P, CT, E]), ALU.mult))
                then(dve.tensor_reduce(expert[:, :], running[:, :, :], X, ALU.add))

            def locate_slots():
                dve.tensor_scalar(keep[:, :], rank[:, :], float(CAP), None, ALU.is_le)
                then(dve.tensor_scalar(past1[:, :], rank[:, :], float(P), None, ALU.is_gt))
                for k in range(2, EB):
                    then(dve.scalar_tensor_tensor(out=past1[:, :], in0=rank[:, :], scalar=float(k * P),
                                                  in1=past1[:, :], op0=ALU.is_gt, op1=ALU.add))
                dve.scalar_tensor_tensor(out=blk_b[:, :], in0=expert[:, :], scalar=float(EB), in1=past1[:, :],
                                         op0=ALU.mult, op1=ALU.add)
                then(dve.scalar_tensor_tensor(out=lo[:, :], in0=past1[:, :], scalar=-float(P), in1=rank[:, :],
                                              op0=ALU.mult, op1=ALU.add))
                then(dve.tensor_tensor(lo[:, :], lo[:, :], keep[:, :], ALU.mult))
                then(dve.tensor_scalar(lo_b[:, :], lo[:, :], -1.0, None, ALU.add))

            def weigh_choices():
                dve.wait_ge(gate_exp, 1)
                then(dve.tensor_scalar(gate_d[:, :], gate_e[:, :], 1.0, None, ALU.add))
                then(dve.reciprocal(gates[:, 0, :], gate_d[:, :]))
                then(dve.tensor_tensor(gates[:, 1, :], gate_e[:, :], gates[:, 0, :], ALU.mult))

            def split_gates():
                flat = gates[:, :, :].rearrange("p c t -> p (c t)")
                then(dve.tensor_copy(vals[:, 2, :], flat))
                then(dve.tensor_tensor(gate_rest[:, :], flat, vals[:, 2, :], ALU.subtract))
                then(dve.tensor_copy(vals[:, 3, :], gate_rest[:, :]))
                then(dve.tensor_tensor(gate_rest[:, :], gate_rest[:, :], vals[:, 3, :], ALU.subtract))
                then(dve.tensor_copy(vals[:, 4, :], gate_rest[:, :]))

            def carry_values(part):
                w, half = slice(part * LC, (part + 1) * LC), part % 2
                at_least(dve, tabled, part - 1)
                at_least(dve, carried_ready, part)
                dve.tensor_tensor(at_lane[:, half, :, :], lane[:, :, :],
                                  lo_b[:, w].unsqueeze(1).to_broadcast([P, P, LC]), ALU.is_equal)
                then(dve.tensor_tensor(at_block[:, :, :], blocks[:, :, :],
                                       blk_b[:, w].unsqueeze(1).to_broadcast([P, NB, LC]), ALU.is_equal))
                dve.tensor_tensor(carried[:, half, :, :, :],
                                  at_block[:, :, :].unsqueeze(1).to_broadcast([P, VALS, NB, LC]),
                                  vals[:, :, w].unsqueeze(2).to_broadcast([P, VALS, NB, LC]), ALU.mult)\
                   .then_inc(carried_ready, 1)

            def read_table():
                dve.wait_ge(tabled, CT // LC)
                then(dve.tensor_copy(table[:, :, :], bank[6][:, 0:VALS * NB].rearrange("p (v n) -> p v n", v=VALS)))
                then(dve.tensor_scalar(used[:, :], table[:, 0, :], 0.5, None, ALU.is_gt))
                then(dve.scalar_tensor_tensor(out=token[:, :], in0=table[:, 0, :], scalar=float(P), in1=table[:, 1, :],
                                              op0=ALU.mult, op1=ALU.add))
                then(dve.tensor_scalar(token[:, :], token[:, :], -float(P), 0.0, ALU.add, ALU.max))
                then(dve.tensor_copy(from_row[:, :], token[:, :]))
                then(dve.tensor_scalar(spare[:, :], p_index_f[:, 0:1].to_broadcast([P, NB]), float(T), None, ALU.add))
                then(dve.tensor_tensor(token[:, :], token[:, :], spare[:, :], ALU.subtract))
                then(dve.tensor_tensor(token[:, :], token[:, :], used[:, :], ALU.mult))
                then(dve.tensor_tensor(to_row[:, :], token[:, :], spare[:, :], ALU.add))
                then(dve.tensor_tensor(slot_gate[:, :], table[:, 2, :], table[:, 3, :], ALU.add))
                dve.tensor_tensor(slot_gate[:, :], slot_gate[:, :], table[:, 4, :], ALU.add).then_inc(table_ready, 1)

            def gate_slot(n, f, width):
                dve.wait_ge(silu_ready, n * FB + (f + 1))
                at_least(dve, down_done, down_count(n - 1))
                dve.tensor_tensor(gated[:, n % 2, f, 0:width], silu[:, f % 2, 0:width],
                                  bank[2 * (f % 2) + 1][:, 0:width], ALU.mult).then_inc(gated_ready, 1)

            def down_count(units):
                return min(units, NC) * CH + max(units - NC, 0) * EB

            def add_shared(n):
                dve.wait_ge(down_done, down_count(n + 1))
                rows = x_sb[:, n * CH:(n + 1) * CH, :]
                dve.tensor_tensor(rows, rows, bank[4 + n % 2][:, :].rearrange("p (k d) -> p k d", k=CH), ALU.add)\
                   .then_inc(summed, 1)

            def scale_slots(e):
                dve.wait_ge(xe_transposed, e + 1)
                at_least(dve, up_done, (NC + e - 1) * FB)
                dve.tensor_scalar(xe_t[:, e % 2, :, :], bank[7][:, 0:EB * P].rearrange("p (k n) -> p k n", k=EB),
                                  g_col[:, 0:1], b_col[:, 0:1], ALU.mult, ALU.add).then_inc(xe_ready, 1)

            def lower_weights(m):
                dve.wait_ge(w_high_ready, m + 1)
                for k in range(2):
                    ins = dve.tensor_tensor(w_low[:, m % 2, k, :], w_float(m)[k], w_high[:, m % 2, k, :].bitcast(F32), ALU.subtract)
                ins.then_inc(w_low_ready, 1)

            for f in range(FB):
                for c in CHUNKS_OF_SLOT[f]:
                    keep_logits(c - 2)
                    scale_chunk(c)
                gate_slot(0, f, CH * P)
                if f == 0:
                    start_token_scales(SPLIT, NT)
                if f == 1:
                    finish_token_scales(SPLIT, NT)
                if f == 2:
                    index_tables()
            keep_logits(NC - 2)
            gate_slot(1, 0, CH * P)
            keep_logits(NC - 1)
            dve.wait_ge(logits_ready, NC)
            largest(0)
            gate_slot(1, 1, CH * P)
            choose(0)
            gate_slot(1, 2, CH * P)
            largest(1)
            gate_slot(1, 3, CH * P)
            choose(1)
            gate_slot(2, 0, CH * P)
            add_shared(0)
            pass_choices()
            gate_slot(2, 1, CH * P)
            gate_slot(2, 2, CH * P)
            sum_tiles(range(0, 3))
            gate_slot(2, 3, CH * P)
            sum_tiles(range(3, E))
            gate_slot(3, 0, CH * P)
            add_shared(1)
            place_choices()
            gate_slot(3, 1, CH * P)
            rank_choices()
            name_experts()
            gate_slot(3, 2, CH * P)
            locate_slots()
            gate_slot(3, 3, CH * P)
            weigh_choices()
            split_gates()
            for slot in range(4 * FB, 6 * FB):
                gate_slot(slot // FB, slot % FB, CH * P)
                if slot % FB == 0:
                    add_shared(slot // FB - 2)
                carry_values(slot - 4 * FB)
            for slot in range(6 * FB, NC * FB):
                gate_slot(slot // FB, slot % FB, CH * P)
                if slot % FB == 0:
                    add_shared(slot // FB - 2)
                if slot == TABLE_SLOT + CT // LC:
                    read_table()
                if slot == FIRST_GATHER_SLOT:
                    scale_slots(0)
                    lower_weights(1)
            lower_unit(NC)

            def gate_output(e, k):
                n = NC + e
                dve.wait_ge(down_done, down_count(n) + k + 1)
                at_least(dve, scattered, 16 * EB * (e - 1))
                s = e * EB + k
                dve.tensor_scalar(ye[:, e % 2, k, :], down_bank(n, k), slot_gate[:, s:s + 1], None,
                                  ALU.mult).then_inc(ye_ready, 1)

            def gate_outputs(e):
                for k in range(EB):
                    gate_output(e, k)

            dve.wait_ge(table_ready, 1)
            for e in range(E):
                n = NC + e
                for f in range(FB):
                    if f == FB - 1 and e + 1 < E:
                        lower_unit(n + 1)
                    gate_slot(n, f, EB * P)
                    if f == 0 and e < 2:
                        add_shared(NC - 2 + e)
                    if f == 0 and e >= 2:
                        gate_outputs(e - 2)
                    if f == 1 and e + 1 < E:
                        scale_slots(e + 1)
                        lower_weights(e + 2)
            gate_outputs(E - 2)
            gate_outputs(E - 1)


def kernel(x, ctx_1024, mask_SxS2_bk0, L0_xattn_Wq, L0_xattn_Wk, L0_xattn_Wv, L0_xattn_Wo, L0_ffn_ln_g, L0_ffn_ln_b,
           L0_ffn_Wr, L0_ffn_W1, L0_ffn_W3, L0_ffn_W2, L0_ffn_W1s, L0_ffn_W3s, L0_ffn_W2s):
    import numpy as np
    import concourse.bacc as bacc
    from concourse.bass_utils import run_bass_kernel_spmd

    given = [x, ctx_1024, mask_SxS2_bk0, L0_xattn_Wq, L0_xattn_Wk, L0_xattn_Wv, L0_xattn_Wo, L0_ffn_ln_g, L0_ffn_ln_b,
             L0_ffn_Wr, L0_ffn_W1, L0_ffn_W3, L0_ffn_W2, L0_ffn_W1s, L0_ffn_W3s, L0_ffn_W2s]
    names = ["x", "ctx", "mask", "wq", "wk", "wv", "wo", "ln_g", "ln_b", "wr", "w1", "w3", "w2", "w1s", "w3s", "w2s"]
    nc = bacc.Bacc("TRN2", target_bir_lowering=False, num_devices=1)
    arrays, args = {}, []
    for name, a in zip(names, given):
        a = np.ascontiguousarray(a)
        arrays[f"in_{name}"] = a
        args.append(nc.dram_tensor(f"in_{name}", a.shape, mybir.dt.from_np(a.dtype), kind="ExternalInput").ap())
    B, S, D = x.shape
    normed = nc.dram_tensor("normed", (B * S, D), F32, kind="Internal").ap()
    out = nc.dram_tensor("out_rows", (B * S + P, D), F32, kind="ExternalOutput").ap()
    xattn_moe(nc, *args, normed, out)
    got = run_bass_kernel_spmd(nc, [arrays], core_ids=[0]).results[0]["out_rows"]
    return got[0:B * S].reshape(B, S, D)
```

```python
from contextlib import ExitStack

import concourse.bass as bass
from concourse import mybir

F32 = mybir.dt.float32
F32R = mybir.dt.float32r
F16 = mybir.dt.float16
BF16 = mybir.dt.bfloat16
I32 = mybir.dt.int32
U32 = mybir.dt.uint32
U8 = mybir.dt.uint8
ALU = mybir.AluOpType
ACT = mybir.ActivationFunctionType
X = mybir.AxisListType.X

P = 128
EPS = 1e-5
CAPACITY_TOKENS = 4 * 256
TOP_K = 2
BANKS = 8
BANK = 512


def at_least(engine, semaphore, value):
    if isinstance(value, int) and value <= 0:
        return
    engine.wait_ge(semaphore, value)


class Chain:

    def __init__(self, engine, semaphore):
        self.engine, self.semaphore, self.count = engine, semaphore, 0

    def then(self, instruction):
        self.count += 1
        instruction.then_inc(self.semaphore, 1)
        self.engine.wait_ge(self.semaphore, self.count)


def xattn_moe(nc, x, ctx, mask, wq, wk, wv, wo, ln_g, ln_b, wr, w1, w3, w2, w1s, w3s, w2s, normed, out):
    B, S, D = x.shape
    T = B * S
    NT = T // P
    H = 16
    HD = D // H
    SCALE = float(HD) ** -0.5
    E, _, F = w1.shape
    FB = F // P
    CAP = -(-5 * CAPACITY_TOKENS * TOP_K // (4 * E))
    EB = -(-CAP // P)
    NB = E * EB
    G = P // 32
    J = H // G
    HH = H // 2
    CH = 4
    NC = NT // CH
    assert S * 2 == P and D == P and HH * S == BANK and NT % (2 * CH) == 0

    x_tiles = x.rearrange("b s d -> (b s) d").rearrange("(t p) d -> p t d", p=P)
    ctx_rows = ctx.rearrange("b s d -> (b s) d")
    normed_tiles = normed.rearrange("(t p) d -> p t d", p=P)
    out_tiles = out[0:T, :].rearrange("(t p) d -> p t d", p=P)

    with ExitStack() as stack:
        def sb(name, shape, dtype=F32):
            return stack.enter_context(nc.sbuf_tensor(name, shape, dtype))

        def sem(name):
            return stack.enter_context(nc.semaphore(name))

        bank = [stack.enter_context(nc.psum_tensor(f"bank{i}", [P, BANK], F32)) for i in range(BANKS)]

        silu = sb("silu", [P, 2, CH * P])
        w_raw = silu[:, 0, :].rearrange("p (n d) -> p n d", n=4)
        w_t = sb("w_t", [P, 4, P])
        wr_sb = sb("wr_sb", [P, E])
        w1_sb = sb("w1_sb", [P, E + 1, F])
        w3_sb = sb("w3_sb", [P, E + 1, F])
        w2_sb = sb("w2_sb", [P, E + 1, FB, D])
        g_col = sb("g_col", [P, 1])
        b_col = sb("b_col", [P, 1])
        ident = sb("ident", [P, P])
        q_select = sb("q_select", [P, 2, S], BF16)
        mask_u8 = sb("mask_u8", [P, S], U8)
        mask_bias = sb("mask_bias", [P, S], BF16)
        row_any = sb("row_any", [P, 1])
        group_mask = sb("group_mask", [P, G, P], F16)
        slot_mask = sb("slot_mask", [P, J, P], F16)
        j_index = silu[:, 1, :].rearrange("p (j n) -> p j n", j=J).bitcast(I32)
        p_index = sb("p_index", [P, 1], I32)
        p_head = sb("p_head", [P, 1], I32)
        p_head_f = sb("p_head_f", [P, 1])
        x_sb = sb("x_sb", [P, NT, D])
        ctx_sb = sb("ctx_sb", [P, 2, D])
        x1_now = sb("x1_now", [P, 2, D])
        stats_now = sb("stats_now", [P, 2, 6])
        stats_all = sb("stats_all", [P, NT, 6])
        sq_sum = sb("sq_sum", [P, NT])
        mean2 = sb("mean2", [P, NT])
        rstd = sb("rstd", [P, NT])
        shift = sb("shift", [P, NT])
        newton = sb("newton", [P, NT])
        variance = sb("variance", [P, NT])
        xn = sb("xn", [P, 2, D])
        x_t = sb("x_t", [P, 2, P])
        ctx_t = sb("ctx_t", [P, 2, 2, 2, S])
        qk_parts = sb("qk_parts", [P, 2, 2, P], F16)
        q_masked = sb("q_masked", [P, 2, 2, G, P], F16)
        k_masked = sb("k_masked", [P, 2, 2, J, P], F16)
        v_block = sb("v_block", [P, 2, 2, H // 2, 2, HD + 1])
        row_max = sb("row_max", [P, 2, HH])
        shifted = sb("shifted", [P, 2, HH, S])
        probs = sb("probs", [P, 2, 2, HH * S])
        probs_t = sb("probs_t", [P, 2, HH // 2, P])
        att_sum = sb("att_sum", [P, H])
        att_inv = sb("att_inv", [P, H])
        att = sb("att", [P, H, HD])
        att_t = sb("att_t", [P, P])
        t_sb = sb("t_sb", [P, 2, CH, D])
        h_t = sb("h_t", [P, NT * P])
        logits = sb("logits", [P, NT, E])
        CT = TOP_K * NT
        by_index = sb("by_index", [P, E])
        e_index = sb("e_index", [P, E])
        top = sb("top", [P, TOP_K, NT])
        eq = sb("eq", [P, NT, E])
        rest = sb("rest", [P, NT, E])
        pick = sb("pick", [P, NT])
        one_hot = sb("one_hot", [P, CT, E])
        one_hot_b = sb("one_hot_b", [P, CT, E], BF16)
        upto = sb("upto", [P, P], BF16)
        ones_b = sb("ones_b", [P, P], BF16)
        zeros = sb("zeros", [P, CT])
        totals = sb("totals", [P, CT, E])
        running = sb("running", [P, CT, E])
        place = sb("place", [P, CT, E])
        rank = sb("rank", [P, CT])
        expert = sb("expert", [P, CT])
        past1 = sb("past1", [P, CT])
        lo = sb("lo", [P, CT])
        keep = sb("keep", [P, CT])
        lo_b = sb("lo_b", [P, CT], BF16)
        blk_b = sb("blk_b", [P, CT], BF16)
        gates = sb("gates", [P, TOP_K, NT])
        gate_e = sb("gate_e", [P, NT])
        gate_d = sb("gate_d", [P, NT])
        LC = 8
        VALS = 5
        vals = sb("vals", [P, VALS, CT], BF16)
        gate_rest = sb("gate_rest", [P, CT])
        lane = sb("lane", [P, P, LC], BF16)
        blocks = sb("blocks", [P, NB, LC], BF16)
        at_lane = sb("at_lane", [P, 2, P, LC], BF16)
        at_block = sb("at_block", [P, NB, LC], BF16)
        carried = sb("carried", [P, 2, VALS, NB, LC], BF16)
        table = sb("table", [P, VALS, NB])
        used = sb("used", [P, NB])
        token = sb("token", [P, NB])
        spare = sb("spare", [P, NB])
        slot_gate = sb("slot_gate", [P, NB])
        from_row = sb("from_row", [P, NB], I32)
        to_row = sb("to_row", [P, NB], I32)
        p_index_f = sb("p_index_f", [P, 1])
        tile_index = sb("tile_index", [P, NT], I32)
        iota_i = sb("iota_i", [P, P], I32)
        zero_rows = sb("zero_rows", [P, D])
        XR = 3
        xe = sb("xe", [P, XR, EB, D])
        xe_t = sb("xe_t", [P, 2, EB, P])
        w_high = sb("w_high", [P, 2, 2, F], F32R)
        w_low = sb("w_low", [P, 2, 2, F], F32R)
        unit_parts = sb("unit_parts", [P, 2, 2, CH * P], F32R)
        gated = sb("gated", [P, 2, FB, CH * P])
        ye = sb("ye", [P, 2, EB, D])

        x_loaded = [sem(f"x_loaded{n}") for n in range(4)]
        w_loaded = sem("w_loaded")
        mask_loaded = sem("mask_loaded")
        small_loaded = sem("small_loaded")
        shared_loaded = sem("shared_loaded")
        experts_loaded = sem("experts_loaded")
        ctx_loaded = [sem("ctx_loaded0"), sem("ctx_loaded1")]
        pool_consts = sem("pool_consts")
        pool_step = sem("pool_step")
        dve_step = sem("dve_step")
        mask_ready = sem("mask_ready")
        w_transposed = sem("w_transposed")
        w_ready = sem("w_ready")
        xn_ready = sem("xn_ready")
        xc_transposed = sem("xc_transposed")
        xc_ready = sem("xc_ready")
        qk_projected = sem("qk_projected")
        qk_high = sem("qk_high")
        qk_low = sem("qk_low")
        qk_masked = sem("qk_masked")
        q_high_spread = sem("q_high_spread")
        x_scaled = sem("x_scaled")
        t_scaled = sem("t_scaled")
        v_projected = sem("v_projected")
        v_placed = sem("v_placed")
        scored = sem("scored")
        max_ready = sem("max_ready")
        shift_ready = sem("shift_ready")
        exp_ready = sem("exp_ready")
        p_transposed = sem("p_transposed")
        p_copied = sem("p_copied")
        att_summed = sem("att_summed")
        att_step = sem("att_step")
        att_ready = sem("att_ready")
        att_transposed = sem("att_transposed")
        att_copied = sem("att_copied")
        att_projected = sem("att_projected")
        x1_ready = sem("x1_ready")
        stats_ready = sem("stats_ready")
        x1_kept = sem("x1_kept")
        t_ready = [sem("t_ready0"), sem("t_ready1")]
        t_stored = [sem("t_stored0"), sem("t_stored1")]
        t_transposed = sem("t_transposed")
        h_ready = sem("h_ready")
        routed = sem("routed")
        logits_ready = sem("logits_ready")
        gate_exp_in = sem("gate_exp_in")
        gate_exp = sem("gate_exp")
        onehot_ready = sem("onehot_ready")
        counted = sem("counted")
        carried_ready = sem("carried_ready")
        tabled = sem("tabled")
        table_ready = sem("table_ready")
        gathered = [sem(f"gathered{e}") for e in range(E)]
        w_high_ready = sem("w_high_ready")
        w_low_ready = sem("w_low_ready")
        w_low_shared = sem("w_low_shared")
        unit_high = sem("unit_high")
        unit_low = sem("unit_low")
        unit_low_shared = sem("unit_low_shared")
        up_done = sem("up_done")
        silu_ready = sem("silu_ready")
        gated_ready = sem("gated_ready")
        down_done = sem("down_done")
        summed = sem("summed")
        zero_ready = sem("zero_ready")
        out_stored = sem("out_stored")
        xe_transposed = sem("xe_transposed")
        xe_ready = sem("xe_ready")
        ye_ready = sem("ye_ready")
        scattered = sem("scattered")

        COUNT_SLOT = 10
        TABLE_SLOT = 18
        FIRST_GATHER_SLOT = 30
        CHUNKS_OF_SLOT = (2, 3), (4,), (5,), (6,), (7,)
        HIDDEN_SLOTS = len(CHUNKS_OF_SLOT)
        assert NC == CHUNKS_OF_SLOT[-1][-1] + 1

        def down_bank(n, k):
            return bank[4 + n % 2][:, k * P:(k + 1) * P] if n < NC else bank[4 + k][:, 0:P]

        def hidden_bank(c):
            return bank[(0, 3)[c] if c < 2 else 5 + c % 2]

        def w_float(m):
            e = m - 1 if m else E
            return w1_sb[:, e, :], w3_sb[:, e, :]

        def unit_width(n):
            return CH * P if n < NC else CAP

        def unit_float(n):
            if n < NC:
                return h_t[:, n * CH * P:(n + 1) * CH * P]
            return xe_t[:, (n - NC) % 2, :, :].rearrange("p k n -> p (k n)")[:, 0:unit_width(n)]

        def unit_part(n, part):
            return unit_parts[:, n % 2, part, 0:unit_width(n)]

        def await_chunk(engine, c):
            engine.wait_ge(t_scaled, 1 if (c + 1) * CH <= SPLIT else 2)
            at_least(engine, t_transposed, c - 1)
            at_least(engine, t_stored[c % 2], c // 2 * 16)

        block = stack.enter_context(nc.Block())

        FIRST, LAST = -3, NT + 3
        LOOP_FROM, LOOP_TO, UNROLLED = 4, NT - 4, 4
        SPLIT = 24

        def pipeline(engine, step, before=None):
            for i in range(FIRST, LOOP_FROM):
                if before and i in before:
                    before[i]()
                step(i, i % 2)
            if before and LOOP_FROM in before:
                before[LOOP_FROM]()
            with engine.Fori(LOOP_FROM // UNROLLED, LOOP_TO // UNROLLED, 1) as steps:
                for k in range(UNROLLED):
                    step(steps * UNROLLED + k, k % 2)
            for i in range(LOOP_TO, LAST):
                if before and i in before:
                    before[i]()
                step(i, i % 2)

        def live(n):
            return not isinstance(n, int) or 0 <= n < NT

        @block.sync
        def _(sp):
            q = NT // 4
            sp.dma_start(x_sb[:, 0:q, :], x_tiles[:, 0:q, :]).then_inc(x_loaded[0], 16)
            for n, w in enumerate((wq, wk, wv, wo)):
                sp.dma_start(w_raw[:, n, :], w).then_inc(w_loaded, 16)
            for n in range(2):
                sp.dma_start(mask_u8[n * S:(n + 1) * S, :], mask).then_inc(mask_loaded, 16)
            for n in range(2):
                sp.dma_start(ctx_sb[:, n, :], ctx_rows[n * P:(n + 1) * P, :]).then_inc(ctx_loaded[n], 16)
            for n in range(1, 4):
                sp.dma_start(x_sb[:, n * q:(n + 1) * q, :], x_tiles[:, n * q:(n + 1) * q, :]).then_inc(x_loaded[n], 16)
            sp.dma_start(g_col[:, :], ln_g.rearrange("(p a) -> p a", a=1)).then_inc(small_loaded, 16)
            sp.dma_start(b_col[:, :], ln_b.rearrange("(p a) -> p a", a=1)).then_inc(small_loaded, 16)
            sp.dma_start(wr_sb[:, :], wr).then_inc(small_loaded, 16)
            sp.dma_start(w1_sb[:, E, :], w1s).then_inc(shared_loaded, 16)
            sp.dma_start(w3_sb[:, E, :], w3s).then_inc(shared_loaded, 16)
            sp.dma_start(w2_sb[:, E, :, :], w2s.rearrange("(f p) d -> p f d", p=P)).then_inc(shared_loaded, 16)

            with sp.Fori(1, NT // 2, 1) as pair:
                for par in range(2):
                    n = pair * 2 + par
                    sp.wait_ge(xc_transposed, n - 1)
                    sp.dma_start(ctx_sb[:, par, :], ctx_rows[bass.ds(n * P, P), :]).then_inc(ctx_loaded[par], 16)
            sp.dma_start(w1_sb[:, 0:E, :], w1.rearrange("e d f -> d e f")).then_inc(experts_loaded, 16)
            sp.dma_start(w3_sb[:, 0:E, :], w3.rearrange("e d f -> d e f")).then_inc(experts_loaded, 16)
            sp.dma_start(w2_sb[:, 0:E, :, :].rearrange("p e f d -> p (e f) d"), w2.rearrange("e (f p) d -> p (e f) d", p=P)).then_inc(experts_loaded, 16)
            with sp.Fori(0, NC // 2, 1) as pair:
                n = pair * 2
                for par in range(2):
                    sp.wait_ge(t_ready[par], pair + 1)
                    sp.dma_start(normed_tiles[:, bass.ds((n + par) * CH, CH), :], t_sb[:, par, :, :])\
                      .then_inc(t_stored[par], 16)
            sp.wait_ge(zero_ready, 1)
            sp.dma_start(out[T:T + P, :], zero_rows[:, :]).then_inc(out_stored, 16)
            with sp.Fori(0, NC, 1) as c:
                sp.wait_ge(summed, c + 1)
                sp.dma_start(out_tiles[:, bass.ds(c * CH, CH), :], x_sb[:, bass.ds(c * CH, CH), :]).then_inc(out_stored, 16)
            sp.wait_ge(scattered, 16 * EB * E)

        @block.gpsimd
        def _(pool):
            def const(ins):
                ins.then_inc(pool_step, 1)

            const(pool.memset(ident[:, :], 0.0))
            pool.wait_ge(pool_step, 1)
            pool.affine_select(out=ident[:, :], in_=ident[:, :], compare_op=ALU.not_equal, fill=1.0, base=0,
                               pattern=[[-1, P]], channel_multiplier=1).then_inc(pool_consts, 1)
            const(pool.memset(v_block[:], 0.0))
            const(pool.memset(group_mask[:], 0.0))
            const(pool.memset(q_masked[:], 0.0))
            const(pool.memset(upto[:, :], 1.0))
            const(pool.memset(mask_bias[:, :], 0.0))
            pool.wait_ge(pool_step, 6)
            done = [1]

            def apart(ins):
                done[0] += 1
                ins.then_inc(pool_consts, 1)
                pool.wait_ge(pool_consts, done[0])

            for half in range(2):
                for par in range(2):
                    for b in range(2):
                        apart(pool.memset(v_block[half * S:(half + 1) * S, par, b, :, half, HD:HD + 1], 1.0))
            for g in range(G):
                apart(pool.memset(group_mask[g * 32:(g + 1) * 32, g, :], 1.0))
            pool.affine_select(out=upto[:, :], in_=upto[:, :], compare_op=ALU.is_ge, fill=0.0, base=0,
                               pattern=[[1, P]], channel_multiplier=-1).then_inc(pool_consts, 1)
            pool.iota(j_index, pattern=[[1, J], [0, P]], base=0, channel_multiplier=0).then_inc(pool_consts, 1)
            pool.iota(p_index[:, :], pattern=[[0, 1]], base=0, channel_multiplier=1).then_inc(pool_consts, 1)
            pool.iota(iota_i[:, :], pattern=[[1, P]], base=0, channel_multiplier=0).then_inc(pool_consts, 1)
            pool.iota(tile_index[:, :], pattern=[[1, NT]], base=1, channel_multiplier=0).then_inc(pool_consts, 1)
            pool.memset(ones_b[:, :], 1.0).then_inc(pool_consts, 1)
            pool.memset(zeros[:, :], 0.0).then_inc(pool_consts, 1)
            pool.memset(zero_rows[:, :], 0.0).then_inc(zero_ready, 1)

            def keep_tile(n, par):
                at_least(pool, stats_ready, n + 1)
                pool.tensor_copy(x_sb[:, bass.ds(n, 1), :].rearrange("p a d -> p (a d)"), x1_now[:, par, :])
                pool.tensor_copy(stats_all[:, bass.ds(n, 1), :].rearrange("p a d -> p (a d)"), stats_now[:, par, :])\
                    .then_inc(x1_kept, 1)

            def normalise_chunk(c):
                await_chunk(pool, c)
                for t in range(c * CH, (c + 1) * CH):
                    ins = pool.tensor_scalar(t_sb[:, c % 2, t % CH, :], x_sb[:, t, :], rstd[:, t:t + 1],
                                             shift[:, t:t + 1], ALU.mult, ALU.add)
                ins.then_inc(t_ready[1], 1)

            def lower_unit(n):
                pool.wait_ge(unit_high, n + 1)
                pool.tensor_tensor(unit_part(n, 1), unit_float(n), unit_part(n, 0).bitcast(F32), ALU.subtract)\
                    .then_inc(unit_low_shared, 1)

            with pool.Fori(0, NT // 2 - 2, 1) as pair:
                keep_tile(pair * 2, 0)
                keep_tile(pair * 2 + 1, 1)
            pool.wait_ge(w_high_ready, 1)
            for k in range(2):
                pool.tensor_tensor(w_low[:, 0, k, :], w_float(0)[k], w_high[:, 0, k, :].bitcast(F32), ALU.subtract)\
                    .then_inc(w_low_shared, 1)
                keep_tile(NT - 4 + k, k)
            keep_tile(NT - 2, 0)
            keep_tile(NT - 1, 1)
            normalise_chunk(3)
            normalise_chunk(5)
            lower_unit(1)
            normalise_chunk(7)
            for n in range(2, NC):
                lower_unit(n)

            pool.wait_ge(table_ready, 1)
            for par in range(2):
                pool.wait_ge(t_stored[par], 16 * (NC // 2))

            def gather(e):
                at_least(pool, xe_transposed, e - XR + 1)
                for k in range(EB):
                    s = e * EB + k
                    pool.indirect_dma_start(xe[:, e % XR, k, :], None, normed,
                                            bass.IndirectOffsetOnAxis(ap=from_row[:, s:s + 1].bitcast(U32), axis=0))\
                        .then_inc(gathered[e], 16)

            for e in range(XR):
                gather(e)
            pool.wait_ge(out_stored, 16 * (NC + 1))
            for e in range(E):
                if e + XR < E:
                    gather(e + XR)
                at_least(pool, scattered, 16 * EB * e)
                for k in range(EB):
                    s = e * EB + k
                    pool.wait_ge(ye_ready, s + 1)
                    pool.indirect_dma_start(out, bass.IndirectOffsetOnAxis(ap=to_row[:, s:s + 1].bitcast(U32), axis=0),
                                            ye[:, e % 2, k, :], None, compute_op=ALU.add).then_inc(scattered, 16)

        POOL_CONSTS = 1 + 8 + G + 1 + 4 + 2

        @block.tensor
        def _(pe):
            pe.wait_ge(pool_consts, 1)
            pe.wait_ge(w_loaded, 64)
            for n in range(4):
                ins = pe.transpose(bank[0][:, n * P:(n + 1) * P], w_raw[:, n, :], ident[:, :])
            ins.then_inc(w_transposed, 1)
            pe.wait_ge(w_ready, 1)

            def transpose_inputs(n, par):
                at_least(pe, qk_low, n)
                pe.wait_ge(ctx_loaded[par], (n // 2 + 1) * 16 if isinstance(n, int) else (n - par) * 8 + 16)
                at_least(pe, xn_ready, n + 1)
                pe.transpose(bank[2][:, 0:P], xn[:, par, :], ident[:, :])
                pe.transpose(bank[2][:, P:2 * P], ctx_sb[:, par, :], ident[:, :]).then_inc(xc_transposed, 1)

            def project_qk(n, par):
                at_least(pe, xc_ready, n + 1)
                pe.matmul(bank[2][:, 2 * P:3 * P], w_t[:, 0, :], x_t[:, par, :], start=True, stop=True)
                pe.matmul(bank[2][:, 3 * P:4 * P], w_t[:, 1, :], ctx_t[:, par, :, 0, :], start=True, stop=True)\
                  .then_inc(qk_projected, 1)

            def project_v(n, par):
                at_least(pe, v_placed, n * 2)
                for b in range(2):
                    ins = pe.matmul(bank[3][:, b * P:(b + 1) * P], ctx_t[:, par, b, :, :].rearrange("p a s -> p (a s)"),
                                    w_t[:, 2, :], start=True, stop=True)
                ins.then_inc(v_projected, 1)

            def score(n, par, half):
                if isinstance(n, int) and n == 0 and half == 0:
                    pe.wait_ge(mask_ready, 1)
                if half == 0:
                    at_least(pe, qk_masked, n + 1)
                    at_least(pe, q_high_spread, n + 1)
                at_least(pe, shift_ready, n * 2 + (half - 1))
                pe.matmul(bank[half][:, :], q_select[:, :, :].rearrange("p b s -> p (b s)"),
                          mask_bias[:, :].unsqueeze(1).to_broadcast([P, HH, S]), start=True, stop=False)
                for gl in range(2):
                    for m, (qp, kp) in enumerate(((0, 0), (0, 1), (1, 0))):
                        for b in range(2):
                            ins = pe.matmul(bank[half][b * S:(b + 1) * S, gl * J * S:(gl + 1) * J * S],
                                            q_masked[:, par, qp, half * 2 + gl, b * S:(b + 1) * S],
                                            k_masked[:, par, kp, :, b * S:(b + 1) * S],
                                            start=False, stop=(gl == 1 and m == 2))
                ins.then_inc(scored, 1)

            def transpose_probs(n, par, half):
                at_least(pe, exp_ready, n * 2 + (half + 1))
                at_least(pe, p_copied, n * 2 + (half - 1))
                for c in range(HH // 2):
                    ins = pe.transpose(bank[4 + half][:, c * P:(c + 1) * P],
                                       probs[:, par, half, c * P:(c + 1) * P], ident[:, :])
                ins.then_inc(p_transposed, 1)

            def weigh_values(n, par, half):
                at_least(pe, p_copied, n * 2 + (half + 1))
                if half == 0:
                    at_least(pe, v_placed, n * 2 + 2)
                    at_least(pe, att_ready, n)
                W = 2 * (HD + 1)
                for c in range(HH // 2):
                    pair = half * (HH // 2) + c
                    for quarter in range(4):
                        rows = slice(quarter * 32, (quarter + 1) * 32)
                        ins = pe.matmul(bank[6][rows, pair * W:(pair + 1) * W], probs_t[:, half, c, rows],
                                        v_block[:, par, quarter // 2, pair, :, :].rearrange("p a d -> p (a d)"),
                                        start=True, stop=True, tile_position=(0, quarter * 32))
                ins.then_inc(att_summed, 1)

            def transpose_att(n):
                at_least(pe, att_ready, n + 1)
                at_least(pe, x1_ready, n)
                pe.transpose(bank[7][:, 0:P], att[:, :, :].rearrange("p h d -> p (h d)"), ident[:, :])\
                  .then_inc(att_transposed, 1)

            def project_out(n):
                at_least(pe, att_copied, n + 1)
                pe.matmul(bank[7][:, P:2 * P], att_t[:, :], w_t[:, 3, :], start=True, stop=True)\
                  .then_inc(att_projected, 1)

            def step(i, par):
                if live(i + 1):
                    project_qk(i + 1, 1 - par)
                if live(i):
                    score(i, par, 0)
                if live(i - 1):
                    transpose_probs(i - 1, 1 - par, 0)
                if live(i + 2):
                    transpose_inputs(i + 2, par)
                if live(i - 1):
                    transpose_probs(i - 1, 1 - par, 1)
                if live(i - 2):
                    transpose_att(i - 2)
                if live(i):
                    score(i, par, 1)
                if live(i - 1):
                    weigh_values(i - 1, 1 - par, 0)
                if live(i - 2):
                    project_out(i - 2)
                if live(i - 1):
                    weigh_values(i - 1, 1 - par, 1)
                if live(i + 1):
                    project_v(i + 1, 1 - par)

            def to_hidden(c):
                pe.wait_ge(t_ready[c % 2], c // 2 + 1)
                if c == 0:
                    pe.wait_ge(shift_ready, NT * 2 - 1)
                elif c == 1:
                    pe.wait_ge(v_placed, NT * 2)
                elif c == 3:
                    pe.wait_ge(att_ready, NT)
                else:
                    pe.wait_ge(h_ready, c - 1)
                for k in range(CH):
                    ins = pe.transpose(hidden_bank(c)[:, k * P:(k + 1) * P], t_sb[:, c % 2, k, :], ident[:, :])
                ins.then_inc(t_transposed, 1)

            def route(c):
                pe.wait_ge(h_ready, c + 1)
                if c == 0:
                    pe.wait_ge(x1_ready, NT)
                at_least(pe, logits_ready, c)
                for k in range(CH):
                    t = c * CH + k
                    for quarter in range(4):
                        row = quarter * 32
                        ins = pe.matmul(bank[7][row:row + 32, k * E:(k + 1) * E], h_t[:, t * P + row:t * P + row + 32],
                                        wr_sb[:, :], start=True, stop=True, tile_position=(0, row))
                ins.then_inc(routed, 1)

            def count_choices():
                pe.wait_ge(onehot_ready, 1)
                flat = one_hot_b[:, :, :].rearrange("p c e -> p (c e)")
                pe.matmul(bank[6][:, 0:CT * E], upto[:, :], flat, start=True, stop=True)
                pe.matmul(bank[7][:, 0:CT * E], ones_b[:, :], flat, start=True, stop=True).then_inc(counted, 1)

            def fill_table(part):
                pe.wait_ge(carried_ready, part + 1)
                for ct in range(part * LC, (part + 1) * LC):
                    half = ct // LC % 2
                    ins = pe.matmul(bank[6][:, 0:VALS * NB], at_lane[:, half, :, ct % LC],
                                    carried[:, half, :, :, ct % LC].rearrange("p v n -> p (v n)"),
                                    start=(ct == 0), stop=(ct == CT - 1))
                ins.then_inc(tabled, 1)

            def up(n, f):
                m = max(n - NC + 1, 0)
                if f == 0:
                    pe.wait_ge(unit_high, n + 1)
                    if n == 0:
                        pe.wait_ge(w_low_shared, 2)
                        pe.wait_ge(unit_low, 1)
                    elif n < NC:
                        pe.wait_ge(unit_low_shared, n)
                    else:
                        pe.wait_ge(w_low_ready, m)
                        pe.wait_ge(unit_low, m + 1)
                at_least(pe, gated_ready, n * FB + (f - 1))
                high, low = unit_part(n, 0), unit_part(n, 1)
                width, columns = high.shape[1], slice(f * P, (f + 1) * P)
                for k in range(2):
                    into = bank[2 * (f % 2) + k][:, 0:width]
                    pe.matmul(into, w_high[:, m % 2, k, columns], high, start=True, stop=False)
                    pe.matmul(into, w_high[:, m % 2, k, columns], low, start=False, stop=False)
                    ins = pe.matmul(into, w_low[:, m % 2, k, columns], high, start=False, stop=True)
                ins.then_inc(up_done, 1)

            def down(n, k, e, tiles):
                if k >= tiles:
                    return
                if k == 0:
                    pe.wait_ge(gated_ready, n * FB + FB)
                if n < NC and k == 0:
                    at_least(pe, summed, n - 1)
                elif n == NC:
                    pe.wait_ge(*((summed, NC - 1), (summed, NC), (table_ready, 1))[k])
                elif n > NC:
                    pe.wait_ge(ye_ready, (n - 1 - NC) * EB + k + 1)
                for f in range(FB):
                    ins = pe.matmul(down_bank(n, k), gated[:, n % 2, f, k * P:(k + 1) * P],
                                    w2_sb[:, e, f, :], start=(f == 0), stop=(f == FB - 1))
                ins.then_inc(down_done, 1)

            def transpose_slots(e):
                pe.wait_ge(gathered[e], 16 * EB)
                at_least(pe, xe_ready, e)
                for k in range(EB):
                    ins = pe.transpose(bank[7][:, k * P:(k + 1) * P], xe[:, e % XR, k, :], ident[:, :])
                ins.then_inc(xe_transposed, 1)

            def shared_slot(n, f):
                up(n, f)
                if n:
                    down(n - 1, f, E, CH)

            def first_slot():
                pe.wait_ge(shared_loaded, 48)
                shared_slot(0, 0)

            pipeline(pe, step, {NT: lambda: to_hidden(0), NT + 1: lambda: to_hidden(1), NT + 2: first_slot})
            for n in range(NC):
                for f in range(FB):
                    slot = n * FB + f
                    if slot:
                        shared_slot(n, f)
                    if slot < HIDDEN_SLOTS:
                        for c in CHUNKS_OF_SLOT[slot]:
                            route(c - 2)
                            to_hidden(c)
                    if slot in (HIDDEN_SLOTS - 1, HIDDEN_SLOTS):
                        route(NC - 1 - HIDDEN_SLOTS + slot)
                    if slot == COUNT_SLOT:
                        count_choices()
                    if TABLE_SLOT <= slot < TABLE_SLOT + CT // LC:
                        fill_table(slot - TABLE_SLOT)
                    if slot == FIRST_GATHER_SLOT:
                        transpose_slots(0)

            pe.wait_ge(experts_loaded, 48)
            for e in range(E):
                for f in range(FB):
                    up(NC + e, f)
                    if e == 0:
                        down(NC - 1, f, E, CH)
                    elif f:
                        down(NC + e - 1, f - 1, e - 1, EB)
                    if f == 1 and e + 1 < E:
                        transpose_slots(e + 1)
            n = NC + E - 1
            for last in range(2):
                pe.wait_ge(gated_ready, n * FB + FB - 1 + last)
                for k in range(EB):
                    pe.wait_ge(ye_ready, (E - 2) * EB + k + 1)
                    for f in (FB - 1,) if last else range(FB - 1):
                        ins = pe.matmul(down_bank(n, k), gated[:, n % 2, f, k * P:(k + 1) * P], w2_sb[:, E - 1, f, :],
                                        start=(f == 0), stop=(f == FB - 1))
                    if last:
                        ins.then_inc(down_done, 1)

        @block.scalar
        def _(act):
            act.wait_ge(w_transposed, 1)
            act.activation(w_t[:, :, :], bank[0][:, :].rearrange("p (n m) -> p n m", n=4), ACT.Copy).then_inc(w_ready, 1)

            def normalise(n, par):
                if isinstance(n, int) and n == 0:
                    act.wait_ge(x_scaled, 1)
                at_least(act, xc_transposed, n - 1)
                act.activation(xn[:, par, :], x_sb[:, bass.ds(n, 1), :].rearrange("p a d -> p (a d)"), ACT.Identity,
                               scale=rstd[:, bass.ds(n, 1)], bias=shift[:, bass.ds(n, 1)]).then_inc(xn_ready, 1)

            def copy_inputs(n, par):
                at_least(act, xc_transposed, n + 1)
                act.activation(x_t[:, par, :], bank[2][:, 0:P], ACT.Copy)
                act.activation(ctx_t[:, par, :, :, :],
                               bank[2][:, P:2 * P].rearrange("p (b s) -> p b s", b=2).unsqueeze(2)
                               .to_broadcast([P, 2, 2, S]), ACT.Copy).then_inc(xc_ready, 1)

            def copy_att(n):
                at_least(act, att_transposed, n + 1)
                act.activation(att_t[:, :], bank[7][:, 0:P], ACT.Copy).then_inc(att_copied, 1)

            def copy_probs(n, half):
                at_least(act, p_transposed, n * 2 + (half + 1))
                at_least(act, att_summed, n * 2 + (half - 1))
                act.activation(probs_t[:, half, :, :], bank[4 + half][:, :].rearrange("p (c n) -> p c n", n=P), ACT.Copy)\
                   .then_inc(p_copied, 1)

            def high_parts(n):
                at_least(act, qk_projected, n + 1)
                at_least(act, qk_masked, n)
                act.activation(qk_parts[:, 0, :, :], bank[2][:, 2 * P:4 * P].rearrange("p (a n) -> p a n", a=2), ACT.Copy)\
                   .then_inc(qk_high, 1)

            def spread_q_high(n, par):
                at_least(act, scored, n * 2 - 2)
                at_least(act, qk_high, n + 1)
                for g in range(G):
                    rows = slice(g * 32, (g + 1) * 32)
                    ins = act.activation(q_masked[rows, par, 0, g, :], qk_parts[rows, 0, 0, :], ACT.Copy)
                ins.then_inc(q_high_spread, 1)

            def exponentials(n, par, half):
                at_least(act, shift_ready, n * 2 + (half + 1))
                act.activation(probs[:, par, half, :], shifted[:, half, :, :].rearrange("p h k -> p (h k)"), ACT.Exp,
                               scale=SCALE).then_inc(exp_ready, 1)

            def place_values(n, par):
                at_least(act, v_projected, n + 1)
                for half in range(2):
                    rows = slice(half * S, (half + 1) * S)
                    ins = act.activation(
                        v_block[rows, par, :, :, half, 0:HD].rearrange("p b h d -> p (b h) d"),
                        bank[3][rows, 0:2 * P].rearrange("p (h a d) -> p h a d", a=2, d=HD)[:, :, half, :], ACT.Copy)
                    ins.then_inc(v_placed, 1)

            def step(i, par):
                if live(i + 1):
                    high_parts(i + 1)
                if live(i - 1):
                    exponentials(i - 1, 1 - par, 1)
                if live(i + 1):
                    spread_q_high(i + 1, 1 - par)
                if live(i - 1):
                    copy_probs(i - 1, 0)
                if live(i + 2):
                    copy_inputs(i + 2, par)
                if live(i - 2):
                    copy_att(i - 2)
                if live(i):
                    place_values(i, par)
                if live(i - 1):
                    copy_probs(i - 1, 1)
                if live(i + 3):
                    normalise(i + 3, 1 - par)
                if live(i):
                    exponentials(i, par, 0)

            def normalise_chunk(c):
                await_chunk(act, c)
                for t in range(c * CH, (c + 1) * CH):
                    ins = act.activation(t_sb[:, c % 2, t % CH, :], x_sb[:, t, :], ACT.Identity,
                                         scale=rstd[:, t:t + 1], bias=shift[:, t:t + 1])
                ins.then_inc(t_ready[c % 2], 1)

            def split_weights(m):
                if m == 0:
                    act.wait_ge(shared_loaded, 48)
                elif m == 1:
                    act.wait_ge(experts_loaded, 48)
                else:
                    act.wait_ge(up_done, (NC + m - 2) * FB)
                for k in range(2):
                    ins = act.activation(w_high[:, m % 2, k, :], w_float(m)[k], ACT.Copy)
                ins.then_inc(w_high_ready, 1)

            def split_unit(n):
                if n < NC:
                    act.wait_ge(h_ready, n + 1)
                else:
                    act.wait_ge(xe_ready, n - NC + 1)
                at_least(act, up_done, (n - 1) * FB)
                act.activation(unit_part(n, 0), unit_float(n), ACT.Copy).then_inc(unit_high, 1)

            def start_unit():
                split_unit(0)
                normalise_chunk(2)

            act.wait_ge(pool_consts, POOL_CONSTS)
            pipeline(act, step, {LOOP_FROM: lambda: act.wait_ge(x_scaled, 2),
                                 NT - 3: lambda: split_weights(0),
                                 NT - 1: lambda: normalise_chunk(0), NT: lambda: normalise_chunk(1),
                                 NT + 1: start_unit})

            def silu_slot(n, f):
                width = unit_width(n)
                act.wait_ge(up_done, n * FB + (f + 1))
                at_least(act, gated_ready, n * FB + (f - 1))
                act.activation(silu[:, f % 2, 0:width], bank[2 * (f % 2)][:, 0:width], ACT.Silu)\
                   .then_inc(silu_ready, 1)

            for f in range(FB):
                silu_slot(0, f)
                if f == 0:
                    normalise_chunk(4)
                if f == 1:
                    split_unit(1)
                    normalise_chunk(6)
            for n in range(1, NC + E):
                when = 1 if n + 1 < NC else 2
                for f in range(FB):
                    if f == when + 1 and n + 1 < NC + E:
                        split_unit(n + 1)
                    silu_slot(n, f)
                    if f == 0 and NC <= n + 1 < NC + E:
                        split_weights(n + 2 - NC)
                if n == 2:
                    act.wait_ge(gate_exp_in, 1)
                    act.activation(gate_e[:, :], gate_d[:, :], ACT.Exp).then_inc(gate_exp, 1)

        @block.vector
        def _(dve):
            chain = Chain(dve, dve_step)
            then = chain.then

            def newton_steps(out_, v, scratch, steps):
                for _ in range(steps):
                    then(dve.tensor_tensor(scratch, out_, out_, ALU.mult))
                    then(dve.scalar_tensor_tensor(out=scratch, in0=scratch, scalar=-0.5, in1=v, op0=ALU.mult, op1=ALU.mult))
                    then(dve.scalar_tensor_tensor(out=out_, in0=scratch, scalar=1.5, in1=out_, op0=ALU.add, op1=ALU.mult))

            def start_scales(tiles, factor, constant):
                even, odd = stats_all[:, tiles, 1], stats_all[:, tiles, 4]
                scratch, root = newton[:, tiles], rstd[:, tiles].bitcast(I32)
                dve.tensor_tensor(sq_sum[:, tiles], stats_all[:, tiles, 2], stats_all[:, tiles, 5], ALU.add)
                dve.tensor_tensor(mean2[:, tiles], even, odd, ALU.add)
                then(dve.tensor_tensor(scratch, even, odd, ALU.subtract))
                then(dve.tensor_tensor(scratch, scratch, scratch, ALU.mult))
                then(dve.scalar_tensor_tensor(out=sq_sum[:, tiles], in0=scratch, scalar=D / 4.0, in1=sq_sum[:, tiles],
                                              op0=ALU.mult, op1=ALU.add))
                then(dve.tensor_scalar(variance[:, tiles], sq_sum[:, tiles], factor / D, constant, ALU.mult, ALU.add))
                then(dve.tensor_scalar(root, variance[:, tiles].bitcast(I32), 1, None, ALU.logical_shift_right))
                then(dve.tensor_scalar(root, root, -1.0, float(0x5f3759df), ALU.mult, ALU.add))

            NEWTON = 3

            def refine_scales(tiles, steps):
                newton_steps(rstd[:, tiles], variance[:, tiles], newton[:, tiles], steps)

            def finish_scales(tiles, steps=NEWTON):
                refine_scales(tiles, steps)
                return dve.scalar_tensor_tensor(out=shift[:, tiles], in0=mean2[:, tiles], scalar=-0.5,
                                                in1=rstd[:, tiles], op0=ALU.mult, op1=ALU.mult)

            def input_stats(first, last):
                for n in range(first, last):
                    ins = dve.bn_stats(stats_all[:, n, :], x_sb[:, n, :])
                then(ins)

            Q = NT // 4
            dve.wait_ge(x_loaded[0], 16)
            input_stats(0, Q)
            start_scales(slice(0, Q), 1.0, EPS)
            finish_scales(slice(0, Q)).then_inc(x_scaled, 1)

            dve.wait_ge(pool_step, 6)
            dve.wait_ge(mask_loaded, 16 * 2)
            then(dve.tensor_scalar(mask_bias[0:S, :], mask_u8[0:S, :], -1.0, 1e9 / SCALE, ALU.add, ALU.mult))
            then(dve.tensor_reduce(row_any[:, :], mask_u8[:, :], X, ALU.max))
            dve.wait_ge(pool_consts, POOL_CONSTS)
            then(dve.tensor_copy(q_select[:, :, :], ident[:, 0:S].unsqueeze(1).to_broadcast([P, 2, S])))
            then(dve.tensor_scalar(p_head[:, :], p_index[:, :], 3, J - 1, ALU.logical_shift_right, ALU.bitwise_and))
            then(dve.tensor_copy(p_head_f[:, :], p_head[:, :]))
            dve.tensor_scalar(slot_mask[:, :, :], j_index[:, :, :], p_head_f[:, 0:1], None, ALU.is_equal)\
               .then_inc(mask_ready, 1)
            dve.wait_ge(mask_ready, 1)

            def find_max(n, half):
                at_least(dve, scored, n * 2 + (half + 1))
                at_least(dve, shift_ready, n * 2 + (half - 1))
                dve.tensor_reduce(row_max[:, half, :], bank[half][:, :].rearrange("p (h k) -> p h k", k=S), X, ALU.max)\
                   .then_inc(max_ready, 1)

            def subtract_max(n, half):
                at_least(dve, max_ready, n * 2 + (half + 1))
                at_least(dve, exp_ready, n * 2 + (half - 1))
                dve.tensor_tensor(shifted[:, half, :, :], bank[half][:, :].rearrange("p (h k) -> p h k", k=S),
                                  row_max[:, half, :].unsqueeze(2).to_broadcast([P, HH, S]), ALU.subtract)\
                   .then_inc(shift_ready, 1)

            def low_parts(n):
                at_least(dve, qk_high, n + 1)
                at_least(dve, qk_masked, n)
                dve.tensor_tensor(qk_parts[:, 1, :, :], bank[2][:, 2 * P:4 * P].rearrange("p (a n) -> p a n", a=2),
                                  qk_parts[:, 0, :, :], ALU.subtract).then_inc(qk_low, 1)

            def spread_q_low(n, par):
                at_least(dve, scored, n * 2 - 2)
                at_least(dve, qk_low, n + 1)
                dve.tensor_tensor(q_masked[:, par, 1, :, :], qk_parts[:, 1, 0, :].unsqueeze(1).to_broadcast([P, G, P]),
                                  group_mask[:, :, :], ALU.mult)

            def spread_k(n, par):
                dve.tensor_tensor(k_masked[:, par, :, :, :],
                                  qk_parts[:, :, 1, :].unsqueeze(2).to_broadcast([P, 2, J, P]),
                                  slot_mask[:, :, :].unsqueeze(1).to_broadcast([P, 2, J, P]), ALU.mult)\
                   .then_inc(qk_masked, 1)

            sums = bank[6][:, 0:H * (HD + 1)].rearrange("p (h d) -> p h d", d=HD + 1)

            def read_sums(n):
                at_least(dve, att_summed, n * 2 + 2)
                at_least(dve, att_ready, n)
                dve.tensor_scalar(att_sum[:, :], sums[:, :, HD], 1e-9, None, ALU.max).then_inc(att_step, 1)

            def invert_sums(n):
                dve.wait_ge(att_step, n * 2 + 1)
                dve.reciprocal(att_inv[:, :], att_sum[:, :]).then_inc(att_step, 1)

            def divide_by_sums(n):
                dve.wait_ge(att_step, n * 2 + 2)
                dve.scalar_tensor_tensor(out=att[:, :, :], in0=sums[:, :, 0:HD], scalar=row_any[:, 0:1],
                                         in1=att_inv[:, :].unsqueeze(2).to_broadcast([P, H, HD]),
                                         op0=ALU.mult, op1=ALU.mult).then_inc(att_ready, 1)

            def add_residual(n, par):
                at_least(dve, att_projected, n + 1)
                at_least(dve, x1_kept, n - 1)
                dve.tensor_tensor(x1_now[:, par, :], x_sb[:, bass.ds(n, 1), :].rearrange("p a d -> p (a d)"),
                                  bank[7][:, P:2 * P], ALU.add).then_inc(x1_ready, 1)

            def take_stats(n, par):
                at_least(dve, x1_ready, n + 1)
                dve.bn_stats(stats_now[:, par, :], x1_now[:, par, :]).then_inc(stats_ready, 1)

            def step(i, par):
                if live(i - 3):
                    add_residual(i - 3, 1 - par)
                if live(i - 2):
                    read_sums(i - 2)
                if live(i + 1):
                    low_parts(i + 1)
                if live(i - 2):
                    invert_sums(i - 2)
                if live(i + 1):
                    spread_q_low(i + 1, 1 - par)
                if live(i - 2):
                    divide_by_sums(i - 2)
                if live(i + 1):
                    spread_k(i + 1, 1 - par)
                if live(i):
                    find_max(i, 0)
                if live(i - 3):
                    take_stats(i - 3, 1 - par)
                if live(i):
                    subtract_max(i, 0)
                    find_max(i, 1)
                    subtract_max(i, 1)

            def start_token_scales(first, last):
                dve.wait_ge(x1_kept, last)
                start_scales(slice(first, last), 1.0 + EPS, EPS * EPS)

            def scale_chunk(c):
                dve.wait_ge(t_transposed, c + 1)
                dve.tensor_scalar(h_t[:, c * CH * P:(c + 1) * CH * P], hidden_bank(c)[:, :], g_col[:, 0:1],
                                  b_col[:, 0:1], ALU.mult, ALU.add).then_inc(h_ready, 1)

            def lower_unit(n):
                dve.wait_ge(unit_high, n + 1)
                dve.tensor_tensor(unit_part(n, 1), unit_float(n), unit_part(n, 0).bitcast(F32), ALU.subtract)\
                   .then_inc(unit_low, 1)

            def place_tables():
                dve.tensor_copy(lane[:, :, :], iota_i[:, :].unsqueeze(2).to_broadcast([P, P, LC]))
                then(dve.tensor_copy(blocks[:, :, :], iota_i[:, 0:NB].unsqueeze(2).to_broadcast([P, NB, LC])))

            def index_tables():
                dve.tensor_copy(e_index[:, :], iota_i[:, 0:E])
                for c in range(TOP_K):
                    dve.tensor_copy(vals[:, 0, c * NT:(c + 1) * NT], tile_index[:, :])
                then(dve.tensor_copy(p_index_f[:, :], p_index[:, :]))
                dve.tensor_scalar(by_index[:, :], e_index[:, :], -1.0, float(E), ALU.mult, ALU.add)
                then(dve.tensor_copy(vals[:, 1, :], p_index_f[:, 0:1].to_broadcast([P, CT])))

            def other_stats(n):
                dve.wait_ge(x_loaded[n], 16)
                input_stats(n * Q, (n + 1) * Q)

            others = slice(Q, NT)

            def first_chunk():
                dve.wait_ge(small_loaded, 16 * 3)
                scale_chunk(0)

            def second_chunk():
                lower_unit(0)
                scale_chunk(1)

            pipeline(dve, step, {-2: lambda: other_stats(1), 0: lambda: other_stats(2), 1: lambda: other_stats(3),
                                 2: lambda: start_scales(others, 1.0, EPS),
                                 3: lambda: finish_scales(others).then_inc(x_scaled, 1),
                                 NT - 4: lambda: start_token_scales(0, SPLIT),
                                 NT - 3: lambda: refine_scales(slice(0, SPLIT), 1),
                                 NT - 2: lambda: finish_scales(slice(0, SPLIT), NEWTON - 1).then_inc(t_scaled, 1),
                                 NT - 1: index_tables,
                                 NT + 1: first_chunk, NT + 2: second_chunk})
            def keep_logits(c):
                dve.wait_ge(routed, c + 1)
                dve.tensor_copy(logits[:, c * CH:(c + 1) * CH, :],
                                bank[7][:, 0:CH * E].rearrange("p (k e) -> p k e", k=CH)).then_inc(logits_ready, 1)

            spread = [P, NT, E]

            def largest(c):
                source = logits
                if c:
                    then(dve.scalar_tensor_tensor(out=rest[:, :, :], in0=one_hot[:, 0:NT, :], scalar=-3e38,
                                                  in1=logits[:, :, :], op0=ALU.mult, op1=ALU.add))
                    source = rest
                then(dve.tensor_reduce(top[:, c, :], source[:, :, :], X, ALU.max))
                then(dve.tensor_tensor(eq[:, :, :], source[:, :, :], top[:, c, :].unsqueeze(2).to_broadcast(spread),
                                       ALU.is_equal))

            def choose(c):
                then(dve.tensor_tensor(eq[:, :, :], eq[:, :, :], by_index[:, :].unsqueeze(1).to_broadcast(spread), ALU.mult))
                then(dve.tensor_reduce(pick[:, :], eq[:, :, :], X, ALU.max))
                then(dve.tensor_tensor(one_hot[:, c * NT:(c + 1) * NT, :], eq[:, :, :],
                                       pick[:, :].unsqueeze(2).to_broadcast(spread), ALU.is_equal))

            def pass_choices():
                dve.tensor_copy(one_hot_b[:, :, :], one_hot[:, :, :]).then_inc(onehot_ready, 1)
                dve.tensor_tensor(gate_d[:, :], top[:, 1, :], top[:, 0, :], ALU.subtract).then_inc(gate_exp_in, 1)

            def sum_tiles(experts):
                if 0 in experts:
                    dve.wait_ge(counted, 1)
                    then(dve.tensor_copy(totals[:, :, :], bank[7][:, 0:CT * E].rearrange("p (c e) -> p c e", e=E)))
                for e in experts:
                    ins = dve.tensor_tensor_scan(running[:, :, e], totals[:, :, e], zeros[:, :], 0.0, ALU.add, ALU.add)
                then(ins)

            def place_choices():
                then(dve.tensor_tensor(running[:, :, :], running[:, :, :], totals[:, :, :], ALU.subtract))
                then(dve.tensor_tensor(place[:, :, :], bank[6][:, 0:CT * E].rearrange("p (c e) -> p c e", e=E),
                                       running[:, :, :], ALU.add))

            def rank_choices():
                then(dve.tensor_tensor(place[:, :, :], place[:, :, :], one_hot[:, :, :], ALU.mult))
                then(dve.tensor_reduce(rank[:, :], place[:, :, :], X, ALU.add))

            def name_experts():
                then(dve.tensor_tensor(running[:, :, :], one_hot[:, :, :],
                                       e_index[:, :].unsqueeze(1).to_broadcast([P, CT, E]), ALU.mult))
                then(dve.tensor_reduce(expert[:, :], running[:, :, :], X, ALU.add))

            def locate_slots():
                dve.tensor_scalar(keep[:, :], rank[:, :], float(CAP), None, ALU.is_le)
                then(dve.tensor_scalar(past1[:, :], rank[:, :], float(P), None, ALU.is_gt))
                for k in range(2, EB):
                    then(dve.scalar_tensor_tensor(out=past1[:, :], in0=rank[:, :], scalar=float(k * P),
                                                  in1=past1[:, :], op0=ALU.is_gt, op1=ALU.add))
                dve.scalar_tensor_tensor(out=blk_b[:, :], in0=expert[:, :], scalar=float(EB), in1=past1[:, :],
                                         op0=ALU.mult, op1=ALU.add)
                then(dve.scalar_tensor_tensor(out=lo[:, :], in0=past1[:, :], scalar=-float(P), in1=rank[:, :],
                                              op0=ALU.mult, op1=ALU.add))
                then(dve.tensor_tensor(lo[:, :], lo[:, :], keep[:, :], ALU.mult))
                then(dve.tensor_scalar(lo_b[:, :], lo[:, :], -1.0, None, ALU.add))

            def weigh_choices():
                dve.wait_ge(gate_exp, 1)
                then(dve.tensor_scalar(gate_d[:, :], gate_e[:, :], 1.0, None, ALU.add))
                then(dve.reciprocal(gates[:, 0, :], gate_d[:, :]))
                then(dve.tensor_tensor(gates[:, 1, :], gate_e[:, :], gates[:, 0, :], ALU.mult))

            def split_gates():
                flat = gates[:, :, :].rearrange("p c t -> p (c t)")
                then(dve.tensor_copy(vals[:, 2, :], flat))
                then(dve.tensor_tensor(gate_rest[:, :], flat, vals[:, 2, :], ALU.subtract))
                then(dve.tensor_copy(vals[:, 3, :], gate_rest[:, :]))
                then(dve.tensor_tensor(gate_rest[:, :], gate_rest[:, :], vals[:, 3, :], ALU.subtract))
                then(dve.tensor_copy(vals[:, 4, :], gate_rest[:, :]))

            def carry_values(part):
                w, half = slice(part * LC, (part + 1) * LC), part % 2
                at_least(dve, tabled, part - 1)
                at_least(dve, carried_ready, part)
                dve.tensor_tensor(at_lane[:, half, :, :], lane[:, :, :],
                                  lo_b[:, w].unsqueeze(1).to_broadcast([P, P, LC]), ALU.is_equal)
                then(dve.tensor_tensor(at_block[:, :, :], blocks[:, :, :],
                                       blk_b[:, w].unsqueeze(1).to_broadcast([P, NB, LC]), ALU.is_equal))
                dve.tensor_tensor(carried[:, half, :, :, :],
                                  at_block[:, :, :].unsqueeze(1).to_broadcast([P, VALS, NB, LC]),
                                  vals[:, :, w].unsqueeze(2).to_broadcast([P, VALS, NB, LC]), ALU.mult)\
                   .then_inc(carried_ready, 1)

            def read_table():
                dve.wait_ge(tabled, CT // LC)
                then(dve.tensor_copy(table[:, :, :], bank[6][:, 0:VALS * NB].rearrange("p (v n) -> p v n", v=VALS)))
                then(dve.tensor_scalar(used[:, :], table[:, 0, :], 0.5, None, ALU.is_gt))
                then(dve.scalar_tensor_tensor(out=token[:, :], in0=table[:, 0, :], scalar=float(P), in1=table[:, 1, :],
                                              op0=ALU.mult, op1=ALU.add))
                then(dve.tensor_scalar(token[:, :], token[:, :], -float(P), 0.0, ALU.add, ALU.max))
                then(dve.tensor_copy(from_row[:, :], token[:, :]))
                then(dve.tensor_scalar(spare[:, :], p_index_f[:, 0:1].to_broadcast([P, NB]), float(T), None, ALU.add))
                then(dve.tensor_tensor(token[:, :], token[:, :], spare[:, :], ALU.subtract))
                then(dve.tensor_tensor(token[:, :], token[:, :], used[:, :], ALU.mult))
                then(dve.tensor_tensor(to_row[:, :], token[:, :], spare[:, :], ALU.add))
                then(dve.tensor_tensor(slot_gate[:, :], table[:, 2, :], table[:, 3, :], ALU.add))
                dve.tensor_tensor(slot_gate[:, :], slot_gate[:, :], table[:, 4, :], ALU.add).then_inc(table_ready, 1)

            def gate_slot(n, f):
                width = unit_width(n)
                dve.wait_ge(silu_ready, n * FB + (f + 1))
                at_least(dve, down_done, down_count(n - 1))
                dve.tensor_tensor(gated[:, n % 2, f, 0:width], silu[:, f % 2, 0:width],
                                  bank[2 * (f % 2) + 1][:, 0:width], ALU.mult).then_inc(gated_ready, 1)

            def down_count(units):
                return min(units, NC) * CH + max(units - NC, 0) * EB

            def add_shared(n):
                dve.wait_ge(down_done, down_count(n + 1))
                rows = x_sb[:, n * CH:(n + 1) * CH, :]
                dve.tensor_tensor(rows, rows, bank[4 + n % 2][:, :].rearrange("p (k d) -> p k d", k=CH), ALU.add)\
                   .then_inc(summed, 1)

            def scale_slots(e):
                dve.wait_ge(xe_transposed, e + 1)
                at_least(dve, up_done, (NC + e - 1) * FB)
                dve.tensor_scalar(xe_t[:, e % 2, :, :], bank[7][:, 0:EB * P].rearrange("p (k n) -> p k n", k=EB),
                                  g_col[:, 0:1], b_col[:, 0:1], ALU.mult, ALU.add).then_inc(xe_ready, 1)

            def lower_weights(m):
                dve.wait_ge(w_high_ready, m + 1)
                for k in range(2):
                    ins = dve.tensor_tensor(w_low[:, m % 2, k, :], w_float(m)[k], w_high[:, m % 2, k, :].bitcast(F32), ALU.subtract)
                ins.then_inc(w_low_ready, 1)

            start_token_scales(SPLIT, NT)
            for slot in range(HIDDEN_SLOTS):
                for c in CHUNKS_OF_SLOT[slot]:
                    keep_logits(c - 2)
                    scale_chunk(c)
                    if c < 1 + NEWTON:
                        refine_scales(slice(SPLIT, NT), 1)
                    elif c == 1 + NEWTON:
                        finish_scales(slice(SPLIT, NT), 1).then_inc(t_scaled, 1)
                gate_slot(slot // FB, slot % FB)
                if slot == HIDDEN_SLOTS - 2:
                    place_tables()
            keep_logits(NC - 2)
            gate_slot(1, 1)
            keep_logits(NC - 1)
            dve.wait_ge(logits_ready, NC)
            largest(0)
            gate_slot(1, 2)
            choose(0)
            largest(1)
            gate_slot(1, 3)
            choose(1)
            gate_slot(2, 0)
            add_shared(0)
            pass_choices()
            gate_slot(2, 1)
            gate_slot(2, 2)
            sum_tiles(range(0, 3))
            gate_slot(2, 3)
            sum_tiles(range(3, E))
            gate_slot(3, 0)
            add_shared(1)
            place_choices()
            gate_slot(3, 1)
            rank_choices()
            name_experts()
            gate_slot(3, 2)
            locate_slots()
            gate_slot(3, 3)
            weigh_choices()
            split_gates()
            for slot in range(4 * FB, 6 * FB):
                gate_slot(slot // FB, slot % FB)
                if slot % FB == 0:
                    add_shared(slot // FB - 2)
                carry_values(slot - 4 * FB)
            for slot in range(6 * FB, NC * FB):
                if slot == NC * FB - 1:
                    lower_unit(NC)
                gate_slot(slot // FB, slot % FB)
                if slot % FB == 0:
                    add_shared(slot // FB - 2)
                if slot == TABLE_SLOT + CT // LC:
                    read_table()
                if slot == FIRST_GATHER_SLOT:
                    scale_slots(0)
                if slot == FIRST_GATHER_SLOT - 1:
                    lower_weights(1)

            def gate_output(e, k):
                n = NC + e
                dve.wait_ge(down_done, down_count(n) + k + 1)
                at_least(dve, scattered, 16 * EB * (e - 1))
                s = e * EB + k
                dve.tensor_scalar(ye[:, e % 2, k, :], down_bank(n, k), slot_gate[:, s:s + 1], None,
                                  ALU.mult).then_inc(ye_ready, 1)

            dve.wait_ge(table_ready, 1)
            for e in range(E):
                n = NC + e
                for f in range(FB):
                    if f == FB - 1 and e + 1 < E:
                        lower_unit(n + 1)
                    gate_slot(n, f)
                    if f == 0 and e < 2:
                        add_shared(NC - 2 + e)
                    if e and 1 <= f <= EB:
                        gate_output(e - 1, f - 1)
                    if f == 1 and e + 1 < E:
                        scale_slots(e + 1)
                        lower_weights(e + 2)
            for k in range(EB):
                gate_output(E - 1, k)


def kernel(x, ctx_1024, mask_SxS2_bk0, L0_xattn_Wq, L0_xattn_Wk, L0_xattn_Wv, L0_xattn_Wo, L0_ffn_ln_g, L0_ffn_ln_b,
           L0_ffn_Wr, L0_ffn_W1, L0_ffn_W3, L0_ffn_W2, L0_ffn_W1s, L0_ffn_W3s, L0_ffn_W2s):
    import numpy as np
    import concourse.bacc as bacc
    from concourse.bass_utils import run_bass_kernel_spmd

    given = [x, ctx_1024, mask_SxS2_bk0, L0_xattn_Wq, L0_xattn_Wk, L0_xattn_Wv, L0_xattn_Wo, L0_ffn_ln_g, L0_ffn_ln_b,
             L0_ffn_Wr, L0_ffn_W1, L0_ffn_W3, L0_ffn_W2, L0_ffn_W1s, L0_ffn_W3s, L0_ffn_W2s]
    names = ["x", "ctx", "mask", "wq", "wk", "wv", "wo", "ln_g", "ln_b", "wr", "w1", "w3", "w2", "w1s", "w3s", "w2s"]
    nc = bacc.Bacc("TRN2", target_bir_lowering=False, num_devices=1)
    arrays, args = {}, []
    for name, a in zip(names, given):
        a = np.ascontiguousarray(a)
        arrays[f"in_{name}"] = a
        args.append(nc.dram_tensor(f"in_{name}", a.shape, mybir.dt.from_np(a.dtype), kind="ExternalInput").ap())
    B, S, D = x.shape
    normed = nc.dram_tensor("normed", (B * S, D), F32, kind="Internal").ap()
    out = nc.dram_tensor("out_rows", (B * S + P, D), F32, kind="ExternalOutput").ap()
    xattn_moe(nc, *args, normed, out)
    got = run_bass_kernel_spmd(nc, [arrays], core_ids=[0]).results[0]["out_rows"]
    return got[0:B * S].reshape(B, S, D)
```
